# Optimizing a Trainium2 kernel written in Bass

```python
import numpy as np
import jax
import jax.numpy as jnp

def _softmax(x, axis=-1):
    return jax.nn.softmax(x, axis=axis)

def _gelu(x):
    return jax.nn.gelu(x, approximate=True)

def _silu(x):
    return jax.nn.silu(x)

def _sigmoid(x):
    return jax.nn.sigmoid(x)

def _layernorm(x, axis=-1, eps=1e-05):
    m = jnp.mean(x, axis=axis, keepdims=True)
    v = jnp.var(x, axis=axis, keepdims=True)
    return (x - m) / jnp.sqrt(v + eps)

def _scatter_add(tgt, idx, src, axis=0):
    return tgt.at[idx].add(src)

def _segment_sum(src, seg, n):
    return jax.ops.segment_sum(src, seg, n)
kernel_name = 'mk_recurrent_d2_jaxref_r8_e2d2df'

def setup_inputs(seed: int=0):
    np.random.seed(seed)
    _w = jnp.asarray

    def _L0_attn_setup():
        import jax, jax.numpy as jnp
        import numpy as np
        B, S, D, H, F = (4, 1024, 128, 16, 64)
        DK = D // H
        EPS = 1e-06

        def _heads(x, W, b):
            y = jnp.einsum('bsd,de->bse', x, W) + b
            return y.reshape(x.shape[0], x.shape[1], H, DK).transpose(0, 2, 1, 3)
        key = jax.random.key(seed)
        ks = jax.random.split(key, 6)
        scale = 1.0 / np.sqrt(D)
        x = jax.random.normal(ks[0], (B, S, D), dtype=jnp.float32)
        Wq = jax.random.normal(ks[1], (D, D), dtype=jnp.float32) * scale
        Wk = jax.random.normal(ks[2], (D, D), dtype=jnp.float32) * scale
        Wv = jax.random.normal(ks[3], (D, D), dtype=jnp.float32) * scale
        Wo = jax.random.normal(ks[4], (D, D), dtype=jnp.float32) * scale
        rw = jax.random.normal(ks[5], (H, DK, F), dtype=jnp.float32) / np.sqrt(DK)
        zb = jnp.zeros((D,), dtype=jnp.float32)
        return {'x': x, 'Wq': Wq, 'bq': zb, 'Wk': Wk, 'bk': zb, 'Wv': Wv, 'bv': zb, 'Wo': Wo, 'bo': zb, 'rw': rw}
    _L0_attn_in = _L0_attn_setup()

    def _L0_ffn_setup():
        import jax, jax.numpy as jnp
        import numpy as np
        NUM_EXPERTS = 8
        TOP_K = 2
        key = jax.random.key(seed)
        ks = jax.random.split(key, 6)
        B, S, D, H, E = (4, 128, 128, 256, NUM_EXPERTS)
        x = jax.random.normal(ks[0], (B, S, D), dtype=jnp.float32)
        Wg = jax.random.normal(ks[1], (D, E), dtype=jnp.float32) * 0.02
        W1 = jax.random.normal(ks[2], (E, D, H), dtype=jnp.float32) * 0.02
        b1 = jax.random.normal(ks[3], (E, H), dtype=jnp.float32) * 0.02
        W2 = jax.random.normal(ks[4], (E, H, D), dtype=jnp.float32) * 0.02
        b2 = jax.random.normal(ks[5], (E, D), dtype=jnp.float32) * 0.02
        return {'x': x, 'Wg': Wg, 'W1': W1, 'b1': b1, 'W2': W2, 'b2': b2}
    _L0_ffn_in = _L0_ffn_setup()

    def _L1_attn_setup():
        import math
        import jax, jax.numpy as jnp
        import numpy as np
        HIDDEN = 128
        HEADS = 16
        HEAD_DIM = HIDDEN // HEADS
        SEQ = 512
        PATCH = 508
        EPS = 1e-06

        def _rms_norm(t, w):
            return t * jax.lax.rsqrt(jnp.mean(t * t, axis=-1, keepdims=True) + EPS) * w

        def _apply_rope(t, cos, sin):
            b, s, h, d = t.shape
            P = cos.shape[0]
            tail = t[:, s - P:].reshape(b, P, h, d // 2, 2)
            x0, x1 = (tail[..., 0], tail[..., 1])
            c = cos[None, :, None, :]
            sn = sin[None, :, None, :]
            rot = jnp.stack([x0 * c - x1 * sn, x0 * sn + x1 * c], axis=-1).reshape(b, P, h, d)
            return jnp.concatenate([t[:, :s - P], rot], axis=1)
        key = jax.random.key(seed)
        ks = jax.random.split(key, 8)
        return {'x': jax.random.normal(ks[0], (1, SEQ, HIDDEN), dtype=jnp.float32), 'rope_cos': jax.random.uniform(ks[1], (PATCH, HEAD_DIM // 2), dtype=jnp.float32), 'rope_sin': jax.random.uniform(ks[2], (PATCH, HEAD_DIM // 2), dtype=jnp.float32), 'wq': jax.random.normal(ks[3], (HIDDEN, HIDDEN), dtype=jnp.float32) / math.sqrt(HIDDEN), 'wk': jax.random.normal(ks[4], (HIDDEN, HIDDEN), dtype=jnp.float32) / math.sqrt(HIDDEN), 'wv': jax.random.normal(ks[5], (HIDDEN, HIDDEN), dtype=jnp.float32) / math.sqrt(HIDDEN), 'wo': jax.random.normal(ks[6], (HIDDEN, HIDDEN), dtype=jnp.float32) / math.sqrt(HIDDEN), 'q_norm_w': jnp.ones((HEAD_DIM,), dtype=jnp.float32), 'k_norm_w': jnp.ones((HEAD_DIM,), dtype=jnp.float32)}
    _L1_attn_in = _L1_attn_setup()

    def _L1_ffn_setup():
        import jax, jax.numpy as jnp
        import numpy as np
        DIM = 128
        INNER = 512
        E = 8
        EPS = 1e-06
        key = jax.random.key(seed)
        k_x, k_wg, k_bg, k_w1, k_w2 = jax.random.split(key, 5)
        x = jax.random.normal(k_x, (4, 256, DIM), dtype=jnp.float32)
        Wg = jax.random.normal(k_wg, (DIM, E), dtype=jnp.float32) / np.sqrt(DIM)
        bg = jax.random.normal(k_bg, (E,), dtype=jnp.float32) * 0.01
        W1 = jax.random.normal(k_w1, (E, DIM, INNER), dtype=jnp.float32) / np.sqrt(DIM)
        W2 = jax.random.normal(k_w2, (E, INNER, DIM), dtype=jnp.float32) / np.sqrt(INNER)
        return {'x': x, 'Wg': Wg, 'bg': bg, 'W1': W1, 'W2': W2}
    _L1_ffn_in = _L1_ffn_setup()
    _d = {'L0_attn_x': _L0_attn_in['x'], 'L0_attn_Wq': _L0_attn_in['Wq'], 'L0_attn_bq': _L0_attn_in['bq'], 'L0_attn_Wk': _L0_attn_in['Wk'], 'L0_attn_bk': _L0_attn_in['bk'], 'L0_attn_Wv': _L0_attn_in['Wv'], 'L0_attn_bv': _L0_attn_in['bv'], 'L0_attn_Wo': _L0_attn_in['Wo'], 'L0_attn_bo': _L0_attn_in['bo'], 'L0_attn_rw': _L0_attn_in['rw'], 'L0_ffn_Wg': _L0_ffn_in['Wg'], 'L0_ffn_W1': _L0_ffn_in['W1'], 'L0_ffn_b1': _L0_ffn_in['b1'], 'L0_ffn_W2': _L0_ffn_in['W2'], 'L0_ffn_b2': _L0_ffn_in['b2'], 'L1_attn_rope_cos': _L1_attn_in['rope_cos'], 'L1_attn_rope_sin': _L1_attn_in['rope_sin'], 'L1_attn_wq': _L1_attn_in['wq'], 'L1_attn_wk': _L1_attn_in['wk'], 'L1_attn_wv': _L1_attn_in['wv'], 'L1_attn_wo': _L1_attn_in['wo'], 'L1_attn_q_norm_w': _L1_attn_in['q_norm_w'], 'L1_attn_k_norm_w': _L1_attn_in['k_norm_w'], 'L1_ffn_Wg': _L1_ffn_in['Wg'], 'L1_ffn_bg': _L1_ffn_in['bg'], 'L1_ffn_W1': _L1_ffn_in['W1'], 'L1_ffn_W2': _L1_ffn_in['W2']}
    _x0 = _d['L0_attn_x']
    _d['L0_attn_x'] = jax.random.normal(jax.random.fold_in(jax.random.key(seed), 1), (2, 2048, 128), dtype=_x0.dtype)
    del _x0
    return _d

def reference(L0_attn_x, L0_attn_Wq, L0_attn_bq, L0_attn_Wk, L0_attn_bk, L0_attn_Wv, L0_attn_bv, L0_attn_Wo, L0_attn_bo, L0_attn_rw, L0_ffn_Wg, L0_ffn_W1, L0_ffn_b1, L0_ffn_W2, L0_ffn_b2, L1_attn_rope_cos, L1_attn_rope_sin, L1_attn_wq, L1_attn_wk, L1_attn_wv, L1_attn_wo, L1_attn_q_norm_w, L1_attn_k_norm_w, L1_ffn_Wg, L1_ffn_bg, L1_ffn_W1, L1_ffn_W2):

    def _L0_attn_ref(x, Wq, bq, Wk, bk, Wv, bv, Wo, bo, rw):
        import jax, jax.numpy as jnp
        import numpy as np
        B, S, D, H, F = (4, 1024, 128, 16, 64)
        DK = D // H
        EPS = 1e-06

        def _heads(x, W, b):
            y = jnp.einsum('bsd,de->bse', x, W) + b
            return y.reshape(x.shape[0], x.shape[1], H, DK).transpose(0, 2, 1, 3)
        q = _heads(x, Wq, bq)
        k = _heads(x, Wk, bk)
        v = _heads(x, Wv, bv)
        qp = jax.nn.relu(jnp.einsum('bhsd,hdf->bhsf', q, rw)) + EPS
        kp = jax.nn.relu(jnp.einsum('bhsd,hdf->bhsf', k, rw)) + EPS
        kv = jnp.einsum('bhsf,bhsd->bhfd', kp, v)
        qkv = jnp.einsum('bhsf,bhfd->bhsd', qp, kv)
        norm = jnp.einsum('bhsf,bhf->bhs', qp, kp.sum(axis=2))
        out = qkv / (norm[..., None] + EPS)
        out = out.transpose(0, 2, 1, 3).reshape(x.shape[0], x.shape[1], D)
        return jnp.einsum('bsd,de->bse', out, Wo) + bo

    def _L0_ffn_ref(x, Wg, W1, b1, W2, b2):
        import jax, jax.numpy as jnp
        import numpy as np
        NUM_EXPERTS = 8
        TOP_K = 2
        B, S, D = x.shape
        E, _, H = W1.shape
        OUT = W2.shape[2]
        xm = x.reshape(-1, D)
        logits = xm @ Wg
        probs = jax.nn.softmax(logits, axis=-1)
        topk_p, topk_i = jax.lax.top_k(probs, TOP_K)
        flat_e = topk_i.reshape(-1)
        flat_p = topk_p.reshape(-1)
        order = jnp.argsort(flat_e)
        tok_idx = order // TOP_K
        e_sorted = flat_e[order]
        p_sorted = flat_p[order]
        xs = xm[tok_idx]
        y = jnp.zeros((xs.shape[0], OUT), dtype=xs.dtype)
        for e in range(E):
            h = jax.nn.relu(xs @ W1[e] + b1[e])
            ye = h @ W2[e] + b2[e]
            m = (e_sorted == e)[:, None].astype(xs.dtype)
            y = y + m * ye
        y = y * p_sorted[:, None]
        out = jnp.zeros((B * S, OUT), dtype=y.dtype).at[tok_idx].add(y)
        return out.reshape(B, S, OUT)

    def _L1_attn_ref(x, rope_cos, rope_sin, wq, wk, wv, wo, q_norm_w, k_norm_w):
        import math
        import jax, jax.numpy as jnp
        import numpy as np
        HIDDEN = 128
        HEADS = 16
        HEAD_DIM = HIDDEN // HEADS
        SEQ = 512
        PATCH = 508
        EPS = 1e-06

        def _rms_norm(t, w):
            return t * jax.lax.rsqrt(jnp.mean(t * t, axis=-1, keepdims=True) + EPS) * w

        def _apply_rope(t, cos, sin):
            b, s, h, d = t.shape
            P = cos.shape[0]
            tail = t[:, s - P:].reshape(b, P, h, d // 2, 2)
            x0, x1 = (tail[..., 0], tail[..., 1])
            c = cos[None, :, None, :]
            sn = sin[None, :, None, :]
            rot = jnp.stack([x0 * c - x1 * sn, x0 * sn + x1 * c], axis=-1).reshape(b, P, h, d)
            return jnp.concatenate([t[:, :s - P], rot], axis=1)
        b, s, _ = x.shape
        q = (x @ wq.T).reshape(b, s, HEADS, HEAD_DIM)
        k = (x @ wk.T).reshape(b, s, HEADS, HEAD_DIM)
        v = (x @ wv.T).reshape(b, s, HEADS, HEAD_DIM)
        q = _rms_norm(q, q_norm_w)
        k = _rms_norm(k, k_norm_w)
        q = _apply_rope(q, rope_cos, rope_sin)
        k = _apply_rope(k, rope_cos, rope_sin)
        q = q / math.sqrt(HEAD_DIM)
        scores = jnp.einsum('bqhd,bkhd->bhqk', q, k)
        attn = jax.nn.softmax(scores.astype(jnp.float32), axis=-1)
        out = jnp.einsum('bhqk,bkhd->bqhd', attn, v).reshape(b, s, HIDDEN)
        return out @ wo.T

    def _L1_ffn_ref(x, Wg, bg, W1, W2):
        import jax, jax.numpy as jnp
        import numpy as np
        DIM = 128
        INNER = 512
        E = 8
        EPS = 1e-06
        B, N, D = x.shape
        num_experts = Wg.shape[1]
        T = B * N
        xf = x.reshape(T, D)
        gate_scores = jax.nn.softmax(xf @ Wg + bg, axis=-1)
        top1 = jnp.argmax(gate_scores, axis=-1)
        mask = jax.nn.one_hot(top1, num_experts, dtype=gate_scores.dtype)
        masked = gate_scores * mask
        denom = masked.sum(axis=0, keepdims=True) + EPS
        gate = masked / denom * T
        gate = gate.reshape(B, N, num_experts)
        out = jnp.zeros((B, N, D), dtype=x.dtype)
        for e in range(num_experts):
            h = jax.nn.relu(jnp.einsum('bnd,dh->bnh', x, W1[e]))
            y = jnp.einsum('bnh,hd->bnd', h, W2[e])
            out = out + gate[..., e:e + 1] * y
        return out
    x = L0_attn_x
    xn = _layernorm(x, axis=-1)
    s = _L0_attn_ref(xn, L0_attn_Wq, L0_attn_bq, L0_attn_Wk, L0_attn_bk, L0_attn_Wv, L0_attn_bv, L0_attn_Wo, L0_attn_bo, L0_attn_rw)
    g = _silu(_L0_ffn_ref(xn, L0_ffn_Wg, L0_ffn_W1, L0_ffn_b1, L0_ffn_W2, L0_ffn_b2))
    x = x + s * g
    xn = _layernorm(x, axis=-1)
    s = _L1_attn_ref(xn, L1_attn_rope_cos, L1_attn_rope_sin, L1_attn_wq, L1_attn_wk, L1_attn_wv, L1_attn_wo, L1_attn_q_norm_w, L1_attn_k_norm_w)
    g = _silu(_L1_ffn_ref(xn, L1_ffn_Wg, L1_ffn_bg, L1_ffn_W1, L1_ffn_W2))
    x = x + s * g
    return x

_drawn_inputs = setup_inputs


def setup_inputs(seed=0):
    import zlib

    import numpy as np

    out = dict(_drawn_inputs(seed))
    spreads = {'L0_attn_bq': (0.0, 0.8),
     'L0_attn_bk': (0.0, 0.8),
     'L0_attn_bv': (0.0, 0.8),
     'L0_attn_bo': (0.0, 0.8),
     'L1_attn_q_norm_w': (1.0, 0.6),
     'L1_attn_k_norm_w': (1.0, 0.6)}
    factors = {'L0_attn_Wq': 8.0,
     'L0_attn_Wk': 8.0,
     'L0_attn_Wv': 8.0,
     'L0_attn_Wo': 8.0,
     'L0_attn_rw': 8.0,
     'L0_ffn_Wg': 8.0,
     'L0_ffn_W1': 8.0,
     'L0_ffn_b1': 8.0,
     'L0_ffn_W2': 8.0,
     'L0_ffn_b2': 8.0,
     'L1_ffn_bg': 3.469,
     'L1_attn_rope_cos': 7.754,
     'L1_attn_rope_sin': 6.711}
    for name, (base, spread) in spreads.items():
        noise = np.random.default_rng([zlib.crc32(name.encode()), seed]).standard_normal(out[name].shape)
        drawn = base * np.exp(spread * noise) if base else spread * noise
        out[name] = jnp.asarray(drawn.astype(out[name].dtype))
    for name, factor in factors.items():
        out[name] = (out[name] * factor).astype(out[name].dtype)
    return out
```

```python
from contextlib import ExitStack

import concourse.bass as bass
from concourse import mybir

F32 = mybir.dt.float32
BF16 = mybir.dt.bfloat16
ALU = mybir.AluOpType
ACT = mybir.ActivationFunctionType
X_AXIS = mybir.AxisListType.X

P = 128
BATCH, SEQ, D = 2, 2048, 128
TOK = BATCH * SEQ
TILES = TOK // P
CHUNK = 512
CHUNKS = TOK // CHUNK
TPC = CHUNK // P
HEADS = 16
DK = D // HEADS
PAIRS = HEADS // 2
FEAT = 64
EXPERTS = 8
LN_EPS = 1e-5
EPS = 1e-6
PARTS = 3
GROUPS = 4
GT = TILES // GROUPS
ROPE = 508

HEAD_ROWS = 64
SHIFT = 32


class Core:
    pass


class Step:

    def __init__(self, turn, per_turn, number):
        self.turn, self.per_turn, self.number = turn, per_turn, number

    def __add__(self, n):
        return Step(self.turn, self.per_turn, self.number + n)

    def at(self, each, more):
        constant = self.number * each + more
        return constant if self.turn is None else self.turn * (self.per_turn * each) + constant


def bc(ap, shape):
    return ap.to_broadcast(shape)


def stage_semaphores(k, ctx, stage):
    nc, taken = k.nc, []

    def clear():
        with nc.Block() as block:
            @block.gpsimd
            def _(pool):
                for semaphore in taken:
                    pool.sem_clear(semaphore)

    def sem(name):
        taken.append(ctx.enter_context(nc.semaphore(stage + name)))
        return taken[-1]

    ctx.callback(clear)
    return sem


def constants(k):
    nc = k.nc
    with ExitStack() as ctx:
        cleared = stage_semaphores(k, ctx, "consts_")("cleared")
        block = ctx.enter_context(nc.Block())

        @block.gpsimd
        def _(pool):
            pool.memset(k.ident[:, :], 0.0).then_inc(cleared, 1)
            pool.memset(k.identb[:, :], 0.0).then_inc(cleared, 1)
            pool.memset(k.expert_rows[:, :, :], 0.0).then_inc(cleared, 1)
            pool.memset(k.ones[:, :], 1.0)
            for ap, value in k.clear:
                pool.memset(ap, value)
            pool.memset(k.sum_parity[:, :], 0.0).then_inc(cleared, 1)
            pool.memset(k.pair_mask[:, :], 0.0).then_inc(cleared, 1)
            pool.memset(k.weight_rank[:, :], 0.0).then_inc(cleared, 1)
            n = 6
            pool.wait_ge(cleared, n)
            for m in (k.ident, k.identb):
                pool.affine_select(out=m[:, :], in_=m[:, :], compare_op=ALU.not_equal, fill=1.0, base=0,
                                   pattern=[[-1, P]], channel_multiplier=1).then_inc(cleared, 1)
            n += 2
            for part in range(PARTS):
                pool.affine_select(out=k.expert_rows[:, :, :], in_=k.expert_rows[:, :, :],
                                   compare_op=ALU.not_equal, fill=1.0, base=-EXPERTS * part,
                                   pattern=[[-1, EXPERTS], [0, P]], channel_multiplier=1).then_inc(cleared, 1)
                n += 1
                pool.wait_ge(cleared, n)
            for group in range(4):
                head = group % 2
                cols = k.sum_parity[:, 9 * head:9 * head + 9]
                pool.affine_select(out=cols, in_=cols, compare_op=ALU.not_equal, fill=1.0, base=-32 * group,
                                   pattern=[[-1, 9]], channel_multiplier=1).then_inc(cleared, 1)
                n += 1
                pool.wait_ge(cleared, n)
            pool.memset(k.pair_mask[0:FEAT, 0:DK], 1.0).then_inc(cleared, 1)
            pool.wait_ge(cleared, n + 1)
            pool.memset(k.pair_mask[FEAT:P, DK:2 * DK], 1.0).then_inc(cleared, 1)
            pool.wait_ge(cleared, n + 2)
            for e in range(EXPERTS):
                pool.memset(k.weight_rank[:, e:e + 1], float(EXPERTS - e))


def normalise(k, tag, x_dram=None):
    nc = k.nc
    x, xnT, bank = k.x, k.xnT, k.bank
    with ExitStack() as ctx:
        sem = stage_semaphores(k, ctx, f"{tag}_")
        xc = ctx.enter_context(nc.sbuf_tensor(f"{tag}_centred", [P, TILES, D], F32))
        sq = ctx.enter_context(nc.sbuf_tensor(f"{tag}_squares", [P, TILES, D], F32))
        st = ctx.enter_context(nc.sbuf_tensor(f"{tag}_stats", [P, 5, TILES], F32))
        total, mean, var, root, rstd = (st[:, i, :] for i in range(5))
        x_in = [sem(f"x_in{g}") for g in range(GROUPS)]
        summed, centred, squared, varred, rooted, scaled, normed, turned, evacuated = (
            sem(n) for n in ("summed", "centred", "squared", "varred", "rooted", "scaled", "normed",
                             "turned", "evacuated"))
        block = ctx.enter_context(nc.Block())

        if x_dram is not None:
            x_tiles = x_dram.rearrange("b (t p) d -> p (b t) d", p=P)

            @block.sync
            def _(sp):
                for g in range(GROUPS):
                    sp.dma_start(x[:, g * GT:(g + 1) * GT, :], x_tiles[:, g * GT:(g + 1) * GT, :]).then_inc(x_in[g], 16)
                k.load_weights(sp)

        def tiles(g):
            return slice(g * GT, (g + 1) * GT)

        @block.vector
        def _(dve):
            def centre(g):
                if x_dram is not None:
                    dve.wait_ge(x_in[g], 16)
                nc.vector.tensor_reduce(total[:, tiles(g)], x[:, tiles(g), :], X_AXIS, ALU.add).then_inc(summed, 1)
                dve.wait_ge(summed, 2 * g + 1)
                nc.vector.tensor_scalar(mean[:, tiles(g)], total[:, tiles(g)], 1.0 / D, None, ALU.mult).then_inc(summed, 1)
                dve.wait_ge(summed, 2 * g + 2)
                nc.vector.tensor_tensor(xc[:, tiles(g), :], x[:, tiles(g), :],
                                        bc(mean[:, tiles(g)].unsqueeze(2), [P, GT, D]), ALU.subtract).then_inc(centred, 1)

            def variance(g):
                dve.wait_ge(squared, g + 1)
                nc.vector.tensor_reduce(total[:, tiles(g)], sq[:, tiles(g), :], X_AXIS, ALU.add).then_inc(varred, 1)
                dve.wait_ge(varred, 2 * g + 1)
                nc.vector.tensor_scalar(var[:, tiles(g)], total[:, tiles(g)], 1.0 / D, LN_EPS, ALU.mult, ALU.add).then_inc(varred, 1)
                dve.wait_ge(rooted, g + 1)
                nc.vector.reciprocal(rstd[:, tiles(g)], root[:, tiles(g)]).then_inc(scaled, 1)

            centre(0)
            for g in range(GROUPS):
                if g + 1 < GROUPS:
                    centre(g + 1)
                variance(g)

        @block.gpsimd
        def _(pool):
            for g in range(GROUPS):
                pool.wait_ge(scaled, g + 1)
                nc.gpsimd.tensor_tensor(sq[:, tiles(g), :], xc[:, tiles(g), :],
                                        bc(rstd[:, tiles(g)].unsqueeze(2), [P, GT, D]), ALU.mult).then_inc(normed, 1)

        @block.scalar
        def _(act):
            def square(g):
                act.wait_ge(centred, g + 1)
                nc.scalar.activation(sq[:, tiles(g), :], xc[:, tiles(g), :], ACT.Square).then_inc(squared, 1)

            square(0)
            for g in range(GROUPS):
                if g + 1 < GROUPS:
                    square(g + 1)
                act.wait_ge(varred, 2 * g + 2)
                nc.scalar.activation(root[:, tiles(g)], var[:, tiles(g)], ACT.Sqrt).then_inc(rooted, 1)
            for c in range(CHUNKS):
                act.wait_ge(turned, c + 1)
                nc.scalar.activation(xnT[:, c * CHUNK:(c + 1) * CHUNK], bank[:, c % 8, :], ACT.Copy).then_inc(evacuated, 1)

        @block.tensor
        def _(pe):
            for c in range(CHUNKS):
                pe.wait_ge(normed, c // 2 + 1)
                for t in range(TPC):
                    mm = nc.tensor.transpose(bank[:, c % 8, t * P:(t + 1) * P], sq[:, c * TPC + t, :], k.ident[:, :])
                mm.then_inc(turned, 1)


def linear_attention(k, w, sT):
    nc = k.nc
    xnT, bank = k.xnT, k.bank
    FR = 8
    with ExitStack() as ctx:
        sem = stage_semaphores(k, ctx, "la_")
        sb = lambda name, shape: ctx.enter_context(nc.sbuf_tensor(f"la_{name}", shape, F32))
        qT = sb("qT", [P, TOK])
        kT = sb("kT", [P, TOK])
        v = sb("v", [P, TILES // BATCH, PAIRS, 32])
        feat = sb("feat", [P, FR, CHUNK])
        kvT = sb("kvT", [P, 2, P])
        num_w = sb("num_w", [P, PAIRS, 32])
        den_w = sb("den_w", [P, PAIRS, 32])
        den = sb("den", [P, CHUNK])
        outT = sb("outT", [P, 4, CHUNK])
        (cleared, q_ready, k_ready, v_ready, q_out, k_out, v_out, feat_ready, feat_out, feat_used,
         kv_out, kvT_ready, weights_out, den_step, out_ready, s_ready, s_out) = (
            sem(n) for n in ("cleared", "q_ready", "k_ready", "v_ready", "q_out", "k_out", "v_out", "feat_ready",
                             "feat_out", "feat_used", "kv_out", "kvT_ready", "weights_out",
                             "den_step", "out_ready", "s_ready", "s_out"))
        block = ctx.enter_context(nc.Block())
        CB = CHUNKS // BATCH
        NF = 2 * TPC * CB
        Q_BANK, K_BANK, V_BANK, F_BANK, KV_BANK, T_BANK = 0, 1, 2, 3, 5, 7
        NUM_BANK, DEN_BANK, S_BANK = (0, 2), (1, 7), 5

        def group_of(b, g):
            return 2 * CB * b + g

        @block.gpsimd
        def _(pool):
            pool.memset(v[:, :, :, :], 0.0).then_inc(cleared, 1)
            pool.wait_ge(cleared, 1)
            pool.memset(v[:, :, :, 2 * DK:2 * DK + 1], 1.0).then_inc(cleared, 1)
            pool.memset(num_w[:, :, :], 0.0).then_inc(cleared, 1)
            pool.memset(den_w[:, :, :], 0.0).then_inc(cleared, 1)

        @block.tensor
        def _(pe):
            pe.wait_ge(cleared, 4)
            k.wait_weights(pe)

            def project(b, c):
                if b > 0 or c > 0:
                    pe.wait_ge(q_out, CB * b + c)
                    pe.wait_ge(k_out, CB * b + c)
                    pe.wait_ge(v_out, CB * b + c)
                at = (CB * b + c) * CHUNK
                nc.tensor.matmul(bank[:, Q_BANK, :], w.Wq[:, :], xnT[:, at:at + CHUNK], start=True, stop=True).then_inc(q_ready, 1)
                nc.tensor.matmul(bank[:, K_BANK, :], w.Wk[:, :], xnT[:, at:at + CHUNK], start=True, stop=True).then_inc(k_ready, 1)
                for t in range(TPC):
                    mm = nc.tensor.matmul(bank[:, V_BANK, t * P:(t + 1) * P], xnT[:, at + t * P:at + (t + 1) * P],
                                          w.Wv[:, :], start=True, stop=True)
                mm.then_inc(v_ready, 1)

            def feature(f, lhsT, rhs):
                if f >= 2:
                    pe.wait_ge(feat_out, f - 1)
                nc.tensor.matmul(bank[:, F_BANK + f % 2, :], lhsT, rhs, start=True, stop=True).then_inc(feat_ready, 1)

            def keys_values(b, i):
                f = 2 * NF * b + i
                tile, half = i // 2, i % 2
                pe.wait_ge(feat_out, f + 1)
                pe.wait_ge(v_out, CB * b + tile // TPC + 1)
                for j in range(4):
                    mm = nc.tensor.matmul(bank[32 * j:32 * j + 32, KV_BANK + half, 0:P], v[:, tile, 4 * half + j, :],
                                          feat[:, f % FR, j * P:(j + 1) * P], start=(tile == 0),
                                          stop=(tile == TILES // BATCH - 1), tile_position=(0, 32 * j))
                mm.then_inc(feat_used, 1)
                return mm

            def quotient(b, g):
                n = group_of(b, g)
                f0 = 2 * NF * b + NF + 4 * g
                pe.wait_ge(feat_out, f0 + 4)
                if n >= 2:
                    pe.wait_ge(out_ready, n - 1)
                for weight, to in ((num_w, NUM_BANK[g % 2]), (den_w, DEN_BANK[g % 2])):
                    for j in range(4):
                        mm = nc.tensor.matmul(bank[32 * j:32 * j + 32, to, :], weight[:, 4 * (g % 2) + j, :],
                                              feat[:, (f0 + j) % FR, :], start=True, stop=True,
                                              tile_position=(0, 32 * j))
                mm.then_inc(feat_used, 4)

            def project_out(b, c):
                n = CB * b + c
                pe.wait_ge(out_ready, 2 * n + 2)
                if n >= 2:
                    pe.wait_ge(s_out, n - 1)
                for half in range(2):
                    mm = nc.tensor.matmul(bank[:, S_BANK + n % 2, :], w.Wo[:, half, :], outT[:, (2 * n + half) % 4, :],
                                          start=(half == 0), stop=(half == 1))
                mm.then_inc(s_ready, 1)

            for b in range(BATCH):
                if b > 0:
                    pe.wait_ge(out_ready, group_of(b, 0))
                    pe.wait_ge(s_out, CB * b)
                for i in range(NF):
                    if i % (2 * TPC) == 0:
                        project(b, i // (2 * TPC))
                        pe.wait_ge(k_out, CB * b + i // (2 * TPC) + 1)
                    at = SEQ * b + (i // 2) * P
                    feature(2 * NF * b + i, kT[:, at:at + P], w.rw[:, (i % 2) * CHUNK:(i % 2 + 1) * CHUNK])
                    if i:
                        keys_values(b, i - 1)
                keys_values(b, NF - 1)
                pe.wait_ge(kv_out, b + 1)
                for half in range(2):
                    mm = nc.tensor.transpose(bank[:, T_BANK, half * P:(half + 1) * P], kvT[:, half, :], k.ident[:, :])
                mm.then_inc(kvT_ready, 1)
                pe.wait_ge(q_out, CB * (b + 1))
                pe.wait_ge(weights_out, 2 * (b + 1))
                for g in range(2 * CB):
                    at = SEQ * b + (g // 2) * CHUNK
                    for j in range(4):
                        pair = 4 * (g % 2) + j
                        feature(2 * NF * b + NF + 4 * g + j, w.rw[:, pair * P:(pair + 1) * P], qT[:, at:at + CHUNK])
                    if g >= 1:
                        quotient(b, g - 1)
                    if g % 2 and g >= 3:
                        project_out(b, (g - 3) // 2)
                quotient(b, 2 * CB - 1)
                project_out(b, CB - 1)

        @block.scalar
        def _(act):
            k.wait_weights(act)
            for b in range(BATCH):
                for c in range(CB):
                    n = CB * b + c
                    act.wait_ge(q_ready, n + 1)
                    nc.scalar.activation(qT[:, n * CHUNK:(n + 1) * CHUNK], bank[:, Q_BANK, :], ACT.Identity,
                                         bias=w.bq[:, :]).then_inc(q_out, 1)
                    act.wait_ge(k_ready, n + 1)
                    nc.scalar.activation(kT[:, n * CHUNK:(n + 1) * CHUNK], bank[:, K_BANK, :], ACT.Identity,
                                         bias=w.bk[:, :]).then_inc(k_out, 1)
                act.wait_ge(feat_used, 2 * NF * b + NF)
                nc.scalar.activation(kvT[:, :, :], bank[:, KV_BANK:KV_BANK + 2, 0:P], ACT.Copy).then_inc(kv_out, 1)
                for c in range(CB):
                    n = CB * b + c
                    act.wait_ge(s_ready, n + 1)
                    nc.scalar.activation(sT[:, n * CHUNK:(n + 1) * CHUNK], bank[:, S_BANK + n % 2, :], ACT.Identity,
                                         bias=w.bo[:, :]).then_inc(s_out, 1)

        @block.vector
        def _(dve):
            k.wait_weights(dve)
            dve.wait_ge(cleared, 4)

            def feature(f):
                dve.wait_ge(feat_ready, f + 1)
                if f >= FR:
                    dve.wait_ge(feat_used, f - FR + 1)
                nc.vector.tensor_scalar(feat[:, f % FR, :], bank[:, F_BANK + f % 2, :], 0.0, EPS, ALU.max, ALU.add).then_inc(feat_out, 1)

            def divide(b, g):
                n = group_of(b, g)
                dve.wait_ge(feat_used, 2 * NF * b + NF + 4 * (g + 1))
                if n:
                    dve.wait_ge(out_ready, n)
                nc.vector.tensor_scalar(den[:, :], bank[:, DEN_BANK[g % 2], :], EPS, None, ALU.add).then_inc(den_step, 1)
                dve.wait_ge(den_step, 2 * n + 1)
                nc.vector.reciprocal(den[:, :], den[:, :]).then_inc(den_step, 1)
                dve.wait_ge(den_step, 2 * n + 2)
                if n >= 4:
                    dve.wait_ge(s_ready, (n - 4) // 2 + 1)
                nc.vector.tensor_tensor(outT[:, n % 4, :], bank[:, NUM_BANK[g % 2], :], den[:, :], ALU.mult).then_inc(out_ready, 1)

            for b in range(BATCH):
                for i in range(NF):
                    if i % (2 * TPC) == 0:
                        c = i // (2 * TPC)
                        dve.wait_ge(v_ready, CB * b + c + 1)
                        nc.vector.tensor_tensor(v[:, c * TPC:(c + 1) * TPC, :, 0:2 * DK],
                                                bank[:, V_BANK, :].rearrange("p (t j e) -> p t j e", t=TPC, j=PAIRS),
                                                bc(w.bv[:, :].rearrange("p (j e) -> p j e", j=PAIRS).unsqueeze(1), [P, TPC, PAIRS, 2 * DK]),
                                                ALU.add).then_inc(v_out, 1)
                    feature(2 * NF * b + i)
                dve.wait_ge(kvT_ready, b + 1)
                turned = bank[:, T_BANK, 0:2 * P].rearrange("p (j e) -> p j e", e=32)
                mask = bc(k.pair_mask[:, :].unsqueeze(1), [P, PAIRS, 2 * DK])
                nc.vector.tensor_tensor(num_w[:, :, 0:2 * DK], turned[:, :, 0:2 * DK], mask, ALU.mult).then_inc(weights_out, 1)
                nc.vector.tensor_tensor(den_w[:, :, 0:2 * DK], bc(turned[:, :, 2 * DK:2 * DK + 1], [P, PAIRS, 2 * DK]), mask, ALU.mult).then_inc(weights_out, 1)
                for g in range(2 * CB):
                    for j in range(4):
                        feature(2 * NF * b + NF + 4 * g + j)
                    if g >= 1:
                        divide(b, g - 1)
                divide(b, 2 * CB - 1)


def gates(k, tag, Wg, gT, gTf, bg=None, top=2):
    nc = k.nc
    bank, xnT = k.bank, k.xnT
    with ExitStack() as ctx:
        sem = stage_semaphores(k, ctx, f"{tag}_")
        sb = lambda name, shape, dt=F32: ctx.enter_context(nc.sbuf_tensor(f"{tag}_{name}", shape, dt))
        p = sb("probs", [P, TILES, EXPERTS])
        left = sb("left", [P, TILES, EXPERTS])
        hot = sb("hot", [P, TILES, EXPERTS])
        mask = sb("mask", [P, TILES, EXPERTS])
        one = sb("one", [P, TILES])
        col = sb("col", [P, EXPERTS])
        parts = sb("parts", [P, TILES, PARTS * EXPERTS], BF16)
        scored, stepped, exped, exp_ready, sum_ready, sum_done, gates_ready, turned, taken = (
            sem(n) for n in ("scored", "stepped", "exped", "exp_ready", "sum_ready", "sum_done", "gates_ready",
                             "turned", "taken"))
        block = ctx.enter_context(nc.Block())
        wide = [P, TILES, EXPERTS]
        LOGIT, SUM, TURN = 0, 1, 2
        per = 1024 // P

        @block.tensor
        def _(pe):
            k.wait_late(pe)
            for t in range(TILES):
                mm = nc.tensor.matmul(bank[:, LOGIT, t * EXPERTS:(t + 1) * EXPERTS], xnT[:, t * P:(t + 1) * P], Wg[:, :],
                                      start=True, stop=True)
            mm.then_inc(scored, 1)
            if top == 1:
                pe.wait_ge(sum_ready, 1)
                nc.tensor.matmul(bank[:, SUM, 0:EXPERTS], k.ones[:, :], col[:, :], start=True, stop=True).then_inc(sum_done, 1)
            pe.wait_ge(gates_ready, 1)
            for t in range(TILES):
                out = bank[:, TURN + t // per, :].bitcast(BF16)[0:PARTS * EXPERTS, (t % per) * P:(t % per + 1) * P]
                mm = nc.tensor.transpose(out, parts[:, t, :], k.identb[:, :])
                if t % per == per - 1:
                    mm.then_inc(turned, 1)

        @block.scalar
        def _(act):
            act.wait_ge(exp_ready, 1)
            nc.scalar.activation(p[:, :, :], left[:, :, :], ACT.Exp).then_inc(exped, 1)
            for n in range(TILES // per):
                act.wait_ge(turned, n + 1)
                src = bank[:, TURN + n, :].bitcast(BF16)[0:PARTS * EXPERTS, :]
                nc.scalar.activation(gT[:, n * per * P:(n + 1) * per * P], src, ACT.Copy).then_inc(taken, 1)
                if gTf is not None:
                    nc.scalar.activation(gTf[:, n * per * P:(n + 1) * per * P], src, ACT.Copy).then_inc(taken, 1)

        @block.vector
        def _(dve):
            n = 0

            def step(ins):
                nonlocal n
                ins.then_inc(stepped, 1)
                n += 1
                dve.wait_ge(stepped, n)

            tt, ts, red = nc.vector.tensor_tensor, nc.vector.tensor_scalar, nc.vector.tensor_reduce
            spread = lambda a: bc(a.unsqueeze(2), wide)
            k.wait_late(dve)
            dve.wait_ge(scored, 1)
            logits = bank[:, LOGIT, 0:TILES * EXPERTS].rearrange("p (t e) -> p t e", e=EXPERTS)
            if bg is not None:
                step(tt(p[:, :, :], logits, bc(bg[:, :].unsqueeze(1), wide), ALU.add))
                logits = p[:, :, :]
            step(red(one[:, :], logits, X_AXIS, ALU.max))
            tt(left[:, :, :], logits, spread(one[:, :]), ALU.subtract).then_inc(exp_ready, 1)
            dve.wait_ge(exped, 1)
            step(red(one[:, :], p[:, :, :], X_AXIS, ALU.add))
            step(nc.vector.reciprocal(one[:, :], one[:, :]))
            step(tt(p[:, :, :], p[:, :, :], spread(one[:, :]), ALU.mult))
            step(nc.vector.tensor_copy(left[:, :, :], p[:, :, :]))
            for turn in range(top):
                step(red(one[:, :], left[:, :, :], X_AXIS, ALU.max))
                step(tt(hot[:, :, :], left[:, :, :], spread(one[:, :]), ALU.is_equal))
                step(tt(hot[:, :, :], hot[:, :, :], bc(k.weight_rank[:, :].unsqueeze(1), wide), ALU.mult))
                step(red(one[:, :], hot[:, :, :], X_AXIS, ALU.max))
                step(tt(hot[:, :, :], hot[:, :, :], spread(one[:, :]), ALU.is_equal))
                if turn == 0:
                    step(nc.vector.tensor_copy(mask[:, :, :], hot[:, :, :]))
                else:
                    step(tt(mask[:, :, :], mask[:, :, :], hot[:, :, :], ALU.add))
                if turn + 1 < top:
                    step(nc.vector.scalar_tensor_tensor(left[:, :, :], hot[:, :, :], -2.0, left[:, :, :], ALU.mult, ALU.add))
            step(tt(p[:, :, :], p[:, :, :], mask[:, :, :], ALU.mult))
            if top == 1:
                red(col[:, :], p[:, :, :].rearrange("p t e -> p e t"), X_AXIS, ALU.add).then_inc(sum_ready, 1)
                dve.wait_ge(sum_done, 1)
                step(ts(col[:, :], bank[:, SUM, 0:EXPERTS], EPS, None, ALU.add))
                step(nc.vector.reciprocal(col[:, :], col[:, :]))
                step(tt(p[:, :, :], p[:, :, :], bc(col[:, :].unsqueeze(1), wide), ALU.mult))
                step(ts(p[:, :, :], p[:, :, :], float(TOK), None, ALU.mult))
            part = lambda i: parts[:, :, i * EXPERTS:(i + 1) * EXPERTS]
            step(nc.vector.tensor_copy(part(0), p[:, :, :]))
            step(tt(left[:, :, :], p[:, :, :], part(0), ALU.subtract))
            step(nc.vector.tensor_copy(part(1), left[:, :, :]))
            tt(part(2), left[:, :, :], part(1), ALU.subtract).then_inc(gates_ready, 1)


def experts(k, tag, W1, W2, gT, hidden, out, b1=None, b2=None, gTf=None):
    nc = k.nc
    bank, xnT = k.bank, k.xnT
    HB = hidden // P
    K = EXPERTS * HB
    R = 4
    with ExitStack() as ctx:
        sem = stage_semaphores(k, ctx, f"{tag}_")
        sb = lambda name, shape, dt=F32: ctx.enter_context(nc.sbuf_tensor(f"{tag}_{name}", shape, dt))
        gs = sb("gate", [P, 2, CHUNK])
        hs = sb("hidden", [P, R, CHUNK])
        hg = sb("gated", [P, R, CHUNK])
        g_ready, g_out, h_ready, h_out, hg_out, hg_used, y_out = (
            sem(n) for n in ("g_ready", "g_out", "h_ready", "h_out", "hg_out", "hg_used", "y_out"))
        block = ctx.enter_context(nc.Block())
        G_BANK, H_BANK, Y_BANK = (1, 2), (3, 4, 5, 7), 6
        LAG = 2
        G_FREE, H_FREE, HG_FREE, USED_FREE, Y_FREE = 2, R, 2 * HB, R, 1

        @block.tensor
        def _(pe):
            k.wait_late(pe)
            with pe.Fori(0, CHUNKS, 1) as i:
                x_in = xnT[:, bass.ds(i * CHUNK, CHUNK)]

                def second(n):
                    if n == 0:
                        pe.wait_ge(y_out, i + Y_FREE)
                        if b2 is not None:
                            nc.tensor.matmul(bank[:, Y_BANK, :], b2[:, :], gTf[:, bass.ds(i * CHUNK, CHUNK)],
                                             start=True, stop=False)
                    pe.wait_ge(hg_out, i * K + (n + 1 + HG_FREE))
                    mm = nc.tensor.matmul(bank[:, Y_BANK, :], W2[:, n, :], hg[:, n % R, :],
                                          start=(n == 0 and b2 is None), stop=(n == K - 1))
                    mm.then_inc(hg_used, 1)

                for n in range(K):
                    e, hb = n // HB, n % HB
                    if hb == 0:
                        pe.wait_ge(g_out, i * EXPERTS + (e - 1 + G_FREE))
                    pe.wait_ge(h_out, i * K + (n - R + 1 + H_FREE))
                    nc.tensor.matmul(bank[:, H_BANK[n % R], :], W1[:, n * P:(n + 1) * P], x_in,
                                     start=True, stop=True).then_inc(h_ready, 1)
                    if hb == 0:
                        nc.tensor.matmul(bank[:, G_BANK[e % 2], :], k.expert_rows[:, e, :], gT[:, bass.ds(i * CHUNK, CHUNK)],
                                         start=True, stop=True).then_inc(g_ready, 1)
                    if n >= LAG:
                        second(n - LAG)
                for n in range(K - LAG, K):
                    second(n)

        @block.scalar
        def _(act):
            k.wait_late(act)
            act.sem_inc(g_out, G_FREE)
            act.sem_inc(h_out, H_FREE)
            act.sem_inc(y_out, Y_FREE)
            with act.Fori(0, CHUNKS, 1) as i:
                for n in range(K):
                    e, hb = n // HB, n % HB
                    if hb == 0:
                        act.wait_ge(g_ready, i * EXPERTS + (e + 1))
                        act.wait_ge(hg_out, i * K + ((e - 1) * HB + HG_FREE))
                        nc.scalar.activation(gs[:, e % 2, :], bank[:, G_BANK[e % 2], :], ACT.Copy).then_inc(g_out, 1)
                    act.wait_ge(h_ready, i * K + (n + 1))
                    act.wait_ge(hg_out, i * K + (n - R + 1 + HG_FREE))
                    if b1 is None:
                        ins = nc.scalar.activation(hs[:, n % R, :], bank[:, H_BANK[n % R], :], ACT.Relu)
                    else:
                        ins = nc.scalar.activation(hs[:, n % R, :], bank[:, H_BANK[n % R], :], ACT.Relu, bias=b1[:, n:n + 1])
                    ins.then_inc(h_out, 1)
                act.wait_ge(hg_used, i * K + (K + USED_FREE))
                nc.scalar.activation(out[:, bass.ds(i * CHUNK, CHUNK)], bank[:, Y_BANK, :], ACT.Silu).then_inc(y_out, 1)

        @block.vector
        def _(dve):
            dve.sem_inc(hg_out, HG_FREE)
            with dve.Fori(0, CHUNKS, 1) as i:
                for n in range(K):
                    e = n // HB
                    dve.wait_ge(g_out, i * EXPERTS + (e + 1 + G_FREE))
                    dve.wait_ge(h_out, i * K + (n + 1 + H_FREE))
                    dve.wait_ge(hg_used, i * K + (n - R + 1 + USED_FREE))
                    nc.vector.tensor_tensor(hg[:, n % R, :], hs[:, n % R, :], gs[:, e % 2, :], ALU.mult).then_inc(hg_out, 1)

        @block.gpsimd
        def _(pool):
            pool.sem_inc(hg_used, USED_FREE)


def add_gated(k, sT, gT):
    nc = k.nc
    bank = k.bank
    with ExitStack() as ctx:
        sem = stage_semaphores(k, ctx, "add_")
        product, turned, added = sem("product"), sem("turned"), sem("added")
        block = ctx.enter_context(nc.Block())

        @block.vector
        def _(dve):
            for c in range(CHUNKS + 1):
                if c < CHUNKS:
                    at = slice(c * CHUNK, (c + 1) * CHUNK)
                    nc.vector.tensor_tensor(sT[:, at], sT[:, at], gT[:, at], ALU.mult).then_inc(product, 1)
                if c:
                    dve.wait_ge(turned, c)
                    x = k.x[:, (c - 1) * TPC:c * TPC, :].rearrange("p t d -> p (t d)")
                    nc.vector.tensor_tensor(x, x, bank[:, (c - 1) % 8, :], ALU.add).then_inc(added, 1)

        @block.tensor
        def _(pe):
            for c in range(CHUNKS):
                pe.wait_ge(product, c + 1)
                for t in range(TPC):
                    at = (c * TPC + t) * P
                    mm = nc.tensor.transpose(bank[:, c % 8, t * P:(t + 1) * P], sT[:, at:at + P], k.ident[:, :])
                mm.then_inc(turned, 1)


SEG = 8
Q_PLACES = dict(first=(0, 8), again=48, second=(16, 8), third=56)
K_PLACES = dict(first=(0, 16), again=56, second=(8, 16), third=48)


def attention_operands(k, b, w, QT, KT, V):
    nc = k.nc
    bank, xnT = k.bank, k.xnT
    NG = SEQ // CHUNK
    with ExitStack() as ctx:
        sem = stage_semaphores(k, ctx, f"op{b}_")
        sb = lambda name, shape, dt=F32: ctx.enter_context(nc.sbuf_tensor(f"op{b}_{name}", shape, dt))
        qk = sb("qk", [P, 2, TPC, HEADS, DK])
        rest = sb("rest", [P, 2, TPC, HEADS, DK])
        rot = sb("rot", [P, 4, 2, TPC, HEADS, DK // 2])
        st = sb("st", [P, 3, 2, TPC, HEADS])
        total, root, rstd = (st[:, i] for i in range(3))
        split = sb("split", [P, 2, TPC, HEADS, HEAD_ROWS], BF16)
        (cleared, projected, squared, stat, rooted, scaled, weighted, turned_q, cast1, left1, cast2, split_ready,
         v_out, turned, taken_a, taken_d) = (
            sem(n) for n in ("cleared", "projected", "squared", "stat", "rooted", "scaled", "weighted", "roped",
                             "cast1", "left1", "cast2", "split_ready", "v_out", "turned", "taken_a", "taken_d"))
        block = ctx.enter_context(nc.Block())
        proj = bank[:, 0:TPC, :]
        qk_psum = [proj[:, :, i * D:(i + 1) * D].rearrange("p t (h e) -> p t h e", e=DK) for i in range(2)]
        flat = lambda t, i: t[:, i].rearrange("p t h e -> p (t h) e")

        @block.tensor
        def _(pe):
            k.wait_late(pe)
            for g in range(NG):
                if g:
                    pe.wait_ge(scaled, 2 * g)
                    pe.wait_ge(v_out, g)
                for t in range(TPC):
                    at = SEQ * b + g * CHUNK + t * P
                    mm = nc.tensor.matmul(bank[:, t, 0:3 * D], xnT[:, at:at + P], w.wqkv[:, :], start=True, stop=True)
                mm.then_inc(projected, 1)
                pe.wait_ge(cleared, 3)
                for i in range(2):
                    pe.wait_ge(split_ready, 2 * g + i + 1)
                    for n in range(PAIRS // 2):
                        m = 8 * g + 4 * i + n
                        if m >= 4:
                            pe.wait_ge(taken_a if m % 2 == 0 else taken_d, (m - 4) // 2 + 1)
                        out = bank[:, 4 + n, :].bitcast(BF16)
                        for j in range(2):
                            for t in range(TPC):
                                mm = nc.tensor.transpose(
                                    out[:, (j * TPC + t) * P:(j * TPC + t + 1) * P],
                                    split[:, i, t, 2 * (2 * n + j):2 * (2 * n + j) + 2, :].rearrange("p h r -> p (h r)"),
                                    k.identb[:, :])
                        mm.then_inc(turned, 1)

        def taken(eng, copy, parity, done):
            def run(g, i):
                for n in range(PAIRS // 2):
                    m = 8 * g + 4 * i + n
                    if m % 2 == parity:
                        eng.wait_ge(turned, m + 1)
                        to = (QT, KT)[i]
                        copy(to[:, 2 * n:2 * n + 2, g * CHUNK:(g + 1) * CHUNK],
                             bank[:, 4 + n, :].bitcast(BF16).rearrange("p (j t) -> p j t", j=2)).then_inc(done, 1)
            return run

        @block.scalar
        def _(act):
            take = taken(act, lambda o, i: nc.scalar.activation(o, i, ACT.Copy), 0, taken_a)
            act.wait_ge(cleared, 3)
            for g in range(NG):
                act.wait_ge(projected, g + 1)
                if g:
                    act.wait_ge(split_ready, 2 * g)
                for i in range(2):
                    nc.scalar.activation(rest[:, i], qk_psum[i], ACT.Square).then_inc(squared, 1)
                nc.scalar.activation(V[:, g * TPC:(g + 1) * TPC, :], proj[:, :, 2 * D:3 * D], ACT.Copy).then_inc(v_out, 1)
                act.wait_ge(stat, 2 * g + 2)
                nc.scalar.activation(root[:, :, :, :], total[:, :, :, :], ACT.Sqrt).then_inc(rooted, 1)
                for i, places in enumerate((Q_PLACES, K_PLACES)):
                    act.wait_ge(turned_q, 2 * g + i + 1)
                    if g:
                        act.wait_ge(turned, 8 * g)
                    at, step = places["first"]
                    s = flat(split, i)
                    src = flat(qk, i)
                    nc.scalar.activation(s[:, :, at:at + 8], src, ACT.Copy).then_inc(cast1, 1)
                    nc.scalar.activation(s[:, :, at + step:at + step + 8], src, ACT.Copy).then_inc(cast1, 1)
                    nc.scalar.activation(s[:, :, places["again"]:places["again"] + 8], src, ACT.Copy).then_inc(cast1, 1)
                for i in range(2):
                    take(g, i)

        @block.gpsimd
        def _(pool):
            pool.memset(split[:, :, :, :, :], 0.0).then_inc(cleared, 1)
            pool.wait_ge(cleared, 1)
            pool.memset(split[:, 1, :, :, SHIFT:SHIFT + PARTS], 1.0).then_inc(cleared, 1)
            pool.memset(rot[:, :, :, :, :, :], 0.0).then_inc(cleared, 1)
            k.wait_late(pool)
            for g in range(NG):
                for i in range(2):
                    pool.wait_ge(scaled, 2 * g + i + 1)
                    n = 3 * (2 * g + i)
                    nc.gpsimd.tensor_tensor(flat(qk, i), flat(qk, i), bc(w.norm_w[:, i, :].unsqueeze(1), [P, TPC * HEADS, DK]),
                                            ALU.mult).then_inc(weighted, 1)
                for i, places in enumerate((Q_PLACES, K_PLACES)):
                    pool.wait_ge(left1, 2 * g + i + 1)
                    at, step = places["second"]
                    s = flat(split, i)
                    nc.gpsimd.tensor_copy(s[:, :, at:at + 8], flat(rest, i)).then_inc(cast2, 1)
                    nc.gpsimd.tensor_copy(s[:, :, at + step:at + step + 8], flat(rest, i)).then_inc(cast2, 1)

        @block.vector
        def _(dve):
            k.wait_late(dve)
            take = taken(dve, nc.vector.tensor_copy, 1, taken_d)
            tt = nc.vector.tensor_tensor
            steps = sem("rope_step")
            n = 0
            dve.wait_ge(cleared, 3)
            for g in range(NG):
                for i in range(2):
                    dve.wait_ge(squared, 2 * g + i + 1)
                    nc.vector.tensor_reduce(total[:, i], rest[:, i], X_AXIS, ALU.add).then_inc(steps, 1)
                    n += 1
                dve.wait_ge(steps, n)
                for i in range(2):
                    nc.vector.tensor_scalar(total[:, i], total[:, i], 1.0 / DK, EPS, ALU.mult, ALU.add).then_inc(stat, 1)
                dve.wait_ge(rooted, g + 1)
                nc.vector.reciprocal(rstd[:, :, :, :], root[:, :, :, :]).then_inc(steps, 1)
                n += 1
                dve.wait_ge(steps, n)
                if g:
                    dve.wait_ge(cast1, 6 * g)
                for i in range(2):
                    tt(qk[:, i], qk_psum[i], bc(rstd[:, i].unsqueeze(3), [P, TPC, HEADS, DK]), ALU.mult).then_inc(scaled, 1)
                for i in range(2):
                    dve.wait_ge(weighted, 2 * g + i + 1)
                    if g == NG - 1:
                        x0 = qk[:, i, :, :, 0:DK:2]
                        x1 = qk[:, i, :, :, 1:DK:2]
                        wide = [P, TPC, HEADS, DK // 2]
                        cos, sin = (bc(r[:, :, :].unsqueeze(2), wide) for r in (w.cos, w.sin))
                        for m, (a, f) in enumerate(((x0, cos), (x1, sin), (x0, sin), (x1, cos))):
                            tt(rot[:, m, i], a, f, ALU.mult).then_inc(steps, 1)
                        n += 4
                        dve.wait_ge(steps, n)
                        tt(x0, rot[:, 0, i], rot[:, 1, i], ALU.subtract).then_inc(steps, 1)
                        tt(x1, rot[:, 2, i], rot[:, 3, i], ALU.add).then_inc(steps, 1)
                        n += 2
                        dve.wait_ge(steps, n)
                    nc.vector.tensor_scalar(qk[:, i], qk[:, i], DK ** -0.5 if i == 0 else 1.0, None, ALU.mult).then_inc(turned_q, 1)
                for i, places in enumerate((Q_PLACES, K_PLACES)):
                    s = flat(split, i)
                    dve.wait_ge(cast1, 6 * g + 3 * i + 3)
                    at = places["first"][0]
                    tt(flat(rest, i), flat(qk, i), s[:, :, at:at + 8], ALU.subtract).then_inc(left1, 1)
                for i, places in enumerate((Q_PLACES, K_PLACES)):
                    s = flat(split, i)
                    dve.wait_ge(cast2, 4 * g + 2 * i + 2)
                    at = places["second"][0]
                    tt(s[:, :, places["third"]:places["third"] + 8], flat(rest, i), s[:, :, at:at + 8],
                       ALU.subtract).then_inc(split_ready, 1)
                for i in range(2):
                    take(g, i)


def softmax_attention(k, b, QT, KT, V, attn):
    nc = k.nc
    bank = k.bank
    NK = SEQ // P
    QC = SEQ // CHUNK
    UNROLL = 2
    S = 2 * NK
    R = 3
    PR = 8
    S_BANK, M_BANK, O_BANK, T_BANK = 0, 3, 6, 7
    HOLD = 4
    with ExitStack() as ctx:
        sem = stage_semaphores(k, ctx, f"at{b}_")
        sb = lambda name, shape, dt=F32: ctx.enter_context(nc.sbuf_tensor(f"at{b}_{name}", shape, dt))
        queries = [sb(f"queries{i}", [P, SEQ], BF16) for i in range(2)]
        keys = [[sb(f"keys{i}{h}", [P, SEQ], BF16) for h in range(2)] for i in range(2)]
        values = [sb(f"values{i}", [P, NK, 2, 32]) for i in range(2)]
        probs = sb("probs", [P, PR, CHUNK])
        tops = sb("tops", [P, 2, 2 * TPC, QC])
        neg = sb("neg", [P, 2 * TPC])
        left = sb("left", [P, 2, 2 * TPC])
        shift = sb("shift", [P, TPC, P], BF16)
        sumsT = sb("sumsT", [P, CHUNK])
        inv = sb("inv", [P, 2 * TPC])
        (cleared, copy_allowed, q_loaded, k_loaded, v_loaded, m_ready, m_out, neg_ready, shift_step, shift_ready, shiftT_ready,
         shift_in, s_ready, p_ready, p_used, sums_out, turned, inv_ready, attn_out, pair_done) = (
            sem(n) for n in ("cleared", "copy_allowed", "q_loaded", "k_loaded", "v_loaded", "m_ready", "m_out", "neg_ready",
                             "shift_step", "shift_ready", "shiftT_ready", "shift_in", "s_ready", "p_ready", "p_used",
                             "sums_out", "turned", "inv_ready", "attn_out", "pair_done"))
        block = ctx.enter_context(nc.Block())
        M_FREE, P_FREE, U_FREE, O_FREE, T_FREE = R, R, PR // 4, 1, 1
        G = 4

        ahead = Core()
        ahead.turn = None

        def two_on(n):
            return Step(ahead.turn, n.per_turn, n.number + 2 - (0 if n.turn is None else n.per_turn))

        def turns(eng, body):
            with eng.Fori(0, PAIRS // UNROLL - 1, 1) as i:
                ahead_i = eng.snap(i + 1)
                for u in range(UNROLL):
                    ahead.turn = ahead_i
                    body(Step(i, UNROLL, u), Step(i, UNROLL * QC, u * QC), u, False)
            ahead.turn = None
            for u in range(UNROLL):
                body(Step(None, 0, PAIRS - UNROLL + u), Step(None, 0, (PAIRS - UNROLL + u) * QC), u, u == UNROLL - 1)

        @block.gpsimd
        def _(pool):
            for par in range(2):
                for h in range(2):
                    other = (1 - h) * HEAD_ROWS
                    pool.memset(keys[par][h][other:other + HEAD_ROWS, :], 0.0).then_inc(cleared, 1)
                    pool.wait_ge(cleared, 2 * par + h + 1)
            for par in range(2):
                pool.memset(values[par][:, :, :, DK + 1:32], 0.0)
                pool.memset(values[par][:, :, :, DK:DK + 1], 1.0)
            pool.memset(shift[:, :, :], 0.0).then_inc(cleared, 1)
            pool.sem_inc(m_out, M_FREE)
            pool.sem_inc(p_ready, P_FREE)
            pool.sem_inc(p_used, U_FREE)
            pool.sem_inc(sums_out, O_FREE)
            pool.sem_inc(attn_out, T_FREE)

            def before_copy():
                pool.sem_inc(copy_allowed, 1)

            def load(pair, par):
                before_copy()
                chosen = lambda t, rows: t[rows, bass.ds(pair.at(1, 0), 1), :].rearrange("p a t -> p (a t)")
                nc.gpsimd.tensor_copy(queries[par][:, :], chosen(QT, slice(0, P))).then_inc(q_loaded, 1)
                pool.wait_ge(q_loaded, pair.at(1, 1))
                for h in range(2):
                    rows = slice(h * HEAD_ROWS, (h + 1) * HEAD_ROWS)
                    before_copy()
                    nc.gpsimd.tensor_copy(keys[par][h][rows, :], chosen(KT, rows)).then_inc(k_loaded, 1)
                    pool.wait_ge(k_loaded, pair.at(2, h + 1))
                before_copy()
                for h in range(2):
                    src = V[:, :, bass.ds(pair.at(2 * DK, h * DK), DK)]
                    nc.gpsimd.tensor_copy(values[par][:, :, h, 0:DK], src).then_inc(v_loaded, 1)

            def parts(m):
                pool.wait_ge(neg_ready, m.at(1, 1))
                if m.turn is not None or m.number > 0:
                    pool.wait_ge(shiftT_ready, m.at(1, 0))
                place = lambda i: shift[:, :, :].rearrange("p t (h r) -> p h t r", h=2)[:, :, :, SHIFT + i]
                src = neg[:, :].rearrange("p (h t) -> p h t", h=2)
                rest = [left[:, i, :].rearrange("p (h t) -> p h t", h=2) for i in range(2)]
                before_copy()
                nc.gpsimd.tensor_copy(place(0), src).then_inc(shift_step, 1)
                pool.wait_ge(shift_step, m.at(4, 1))
                nc.gpsimd.tensor_tensor(rest[0], src, place(0), ALU.subtract).then_inc(shift_step, 1)
                pool.wait_ge(shift_step, m.at(4, 2))
                before_copy()
                nc.gpsimd.tensor_copy(place(1), rest[0]).then_inc(shift_step, 1)
                pool.wait_ge(shift_step, m.at(4, 3))
                nc.gpsimd.tensor_tensor(rest[1], rest[0], place(1), ALU.subtract).then_inc(shift_step, 1)
                pool.wait_ge(shift_step, m.at(4, 4))
                before_copy()
                nc.gpsimd.tensor_copy(place(2), rest[1]).then_inc(shift_ready, 1)

            pool.wait_ge(cleared, 5)
            load(Step(None, 0, 0), 0)
            parts(Step(None, 0, 0))

            def pair_steps(pair, chunk, par, final):
                for c in range(QC):
                    if not (final and c == QC - 1):
                        parts(chunk + (c + 1))
                    if c == 0 and not final:
                        pool.wait_ge(p_used, pair.at(QC * S // G, U_FREE))
                        load(pair + 1, 1 - par)

            turns(pool, pair_steps)

        def earlier(s):
            return next(d for d in range(1, 2 * R + 1) if (s - d) % S % R == s % R and (s >= d or (s - d + S) % R == s % R))

        @block.tensor
        def _(pe):
            pe.wait_ge(cleared, 5)

            def for_maxima(m, c, par, a):
                h, qt, kb = a // (TPC * QC), a // QC % TPC, a % QC
                pe.wait_ge(m_out, m.at(S, a - earlier(a) + 1 + M_FREE))
                at = (c * TPC + qt) * P
                nc.tensor.matmul(bank[:, M_BANK + a % R, :], queries[par][:, at:at + P],
                                 keys[par][h][:, kb * CHUNK:(kb + 1) * CHUNK], start=True, stop=True).then_inc(m_ready, 1)

            def shifts(m):
                pe.wait_ge(shift_ready, m.at(1, 1))
                if m.turn is not None or m.number > 1:
                    pe.wait_ge(attn_out, m.at(1, T_FREE - 1))
                out = bank[:, T_BANK, :].bitcast(BF16)
                for t in range(TPC):
                    mm = nc.tensor.transpose(out[:, t * P:(t + 1) * P], shift[:, t, :], k.identb[:, :])
                mm.then_inc(shiftT_ready, 1)

            pe.wait_ge(q_loaded, 1)
            pe.wait_ge(k_loaded, 2)
            for m in range(2):
                for a in range(S):
                    for_maxima(Step(None, 0, m), m, 0, a)
            shifts(Step(None, 0, 0))

            def pair_steps(pair, chunk, par, final):
                for c in range(QC):
                    n = chunk + c
                    more = not (final and c >= QC - 2)
                    m_par = par if c < QC - 2 else 1 - par
                    if c == 0:
                        pe.wait_ge(v_loaded, pair.at(2, 2))
                    if c == QC - 2 and more:
                        pe.wait_ge(q_loaded, pair.at(1, 2))
                        pe.wait_ge(k_loaded, pair.at(2, 4))
                    pe.wait_ge(shift_in, n.at(2, 2))
                    pending = list(range(S)) if more else []

                    def maxima(count):
                        for _ in range(min(count, len(pending))):
                            for_maxima(two_on(n), (c + 2) % QC, m_par, pending.pop(0))

                    def weigh(g):
                        if g == 0:
                            pe.wait_ge(sums_out, n.at(1, O_FREE))
                        pe.wait_ge(p_ready, n.at(S, 4 * g + 4 + P_FREE))
                        for j in range(G):
                            s = G * g + j
                            mm = nc.tensor.matmul(bank[32 * j:32 * j + 32, O_BANK, :], values[par][:, s // 2, s % 2, :],
                                                  probs[:, s % PR, :], start=(g == 0), stop=(g == S // G - 1),
                                                  tile_position=(0, 32 * j))
                        mm.then_inc(p_used, 1)
                        return mm

                    for g in range(S // G):
                        for j in range(G):
                            s = G * g + j
                            pe.wait_ge(p_ready, n.at(S, s - earlier(s) + 1 + P_FREE))
                            nc.tensor.matmul(bank[:, S_BANK + s % R, :], keys[par][s % 2][:, (s // 2) * P:(s // 2 + 1) * P],
                                             queries[par][:, c * CHUNK:(c + 1) * CHUNK], start=True, stop=True).then_inc(s_ready, 1)
                            if j < G - 1:
                                maxima(1)
                        if g > 0:
                            weigh(g - 1)
                        if g == 3 and not (final and c == QC - 1):
                            shifts(n + 1)
                    maxima(4)
                    weigh(S // G - 1)
                    maxima(S)
                    pe.wait_ge(attn_out, n.at(1, T_FREE))
                    pe.wait_ge(sums_out, n.at(1, 1 + O_FREE))
                    for t in range(TPC):
                        mm = nc.tensor.matmul(bank[:, T_BANK, 256 + 18 * t:256 + 18 * (t + 1)], sumsT[:, t * P:(t + 1) * P],
                                              k.sum_parity[:, :], start=True, stop=True)
                    mm.then_inc(turned, 1)

            turns(pe, pair_steps)

        @block.scalar
        def _(act):
            def take_shifts(m, par, c):
                act.wait_ge(shiftT_ready, m.at(1, 1))
                for h in range(2):
                    rows = slice(h * HEAD_ROWS + SHIFT, h * HEAD_ROWS + SHIFT + PARTS)
                    nc.scalar.activation(queries[par][rows, c * CHUNK:(c + 1) * CHUNK],
                                         bank[rows, T_BANK, 0:CHUNK // 2].bitcast(BF16), ACT.Copy).then_inc(shift_in, 1)

            take_shifts(Step(None, 0, 0), 0, 0)

            def pair_steps(pair, chunk, par, final):
                for c in range(QC):
                    n = chunk + c
                    for s in range(S):
                        act.wait_ge(s_ready, n.at(S, s + 1))
                        if s % G == 0:
                            act.wait_ge(p_used, n.at(S // G, s // G - 1 + U_FREE))
                        nc.scalar.activation(probs[:, s % PR, :], bank[:, S_BANK + s % R, :], ACT.Exp).then_inc(p_ready, 1)
                        if s == S * 5 // 8 and not (final and c == QC - 1):
                            take_shifts(n + 1, par if c < QC - 1 else 1 - par, (c + 1) % QC)
                    act.wait_ge(p_used, n.at(S // G, S // G + U_FREE))
                    nc.scalar.activation(sumsT[:, :], bank[:, O_BANK, :], ACT.Copy).then_inc(sums_out, 1)

            turns(act, pair_steps)

        @block.vector
        def _(dve):
            def maxima(m):
                for a in range(S):
                    dve.wait_ge(m_ready, m.at(S, a + 1))
                    nc.vector.tensor_reduce(tops[:, m.number % 2, a // QC, a % QC:a % QC + 1], bank[:, M_BANK + a % R, :], X_AXIS,
                                            ALU.max).then_inc(m_out, 1)
                if m.turn is not None or m.number > 0:
                    dve.wait_ge(shift_ready, m.at(1, 0))
                dve.wait_ge(m_out, m.at(S, S + M_FREE))
                nc.vector.tensor_reduce(neg[:, :], tops[:, m.number % 2], X_AXIS, ALU.max, negate=True).then_inc(neg_ready, 1)

            for m in range(2):
                maxima(Step(None, 0, m))

            def pair_steps(pair, chunk, par, final):
                for c in range(QC):
                    n = chunk + c
                    if not (final and c >= QC - 2):
                        maxima(n + 2)
                    dve.wait_ge(turned, n.at(1, 1))
                    sums = bank[:, T_BANK, 256:256 + 18 * TPC].rearrange("p (t h e) -> p t h e", h=2, e=DK + 1)
                    nc.vector.reciprocal(inv[:, :].rearrange("p (t h) -> p t h", h=2), sums[:, :, :, DK]).then_inc(inv_ready, 1)
                    dve.wait_ge(inv_ready, n.at(1, 1))
                    to = attn[:, c * TPC:(c + 1) * TPC, bass.ds(pair.at(2 * DK, 0), 2 * DK)]
                    nc.vector.tensor_tensor(to.rearrange("p t (h e) -> p t h e", h=2), sums[:, :, :, 0:DK],
                                            bc(inv[:, :].rearrange("p (t h) -> p t h", h=2).unsqueeze(3), [P, TPC, 2, DK]),
                                            ALU.mult).then_inc(attn_out, 1)

            turns(dve, pair_steps)


def finish(k, b, w, attn, gT, out_dram):
    nc = k.nc
    bank = k.bank
    NG = SEQ // CHUNK
    with ExitStack() as ctx:
        sem = stage_semaphores(k, ctx, f"fin{b}_")
        sb = lambda name, shape: ctx.enter_context(nc.sbuf_tensor(f"fin{b}_{name}", shape, F32))
        attnT = sb("attnT", [P, NG, CHUNK])
        product = sb("product", [P, NG, CHUNK])
        turned, taken, projected, gated, back, added, stored = (
            sem(n) for n in ("turned", "taken", "projected", "gated", "back", "added", "stored"))
        block = ctx.enter_context(nc.Block())
        out_tiles = out_dram.rearrange("b (t p) d -> p (b t) d", p=P)

        @block.tensor
        def _(pe):
            for c in range(NG + 2):
                if c < NG:
                    for t in range(TPC):
                        mm = nc.tensor.transpose(bank[:, c % 2, t * P:(t + 1) * P], attn[:, c * TPC + t, :], k.ident[:, :])
                        if c >= 2 and t == 0:
                            pass
                    mm.then_inc(turned, 1)
                if 0 <= c - 1 < NG:
                    pe.wait_ge(taken, c)
                    nc.tensor.matmul(bank[:, 2 + (c - 1) % 2, :], w.woT[:, :], attnT[:, c - 1, :], start=True, stop=True).then_inc(projected, 1)
                if c >= 2:
                    pe.wait_ge(gated, c - 1)
                    for t in range(TPC):
                        mm = nc.tensor.transpose(bank[:, 4 + (c - 2), t * P:(t + 1) * P], product[:, c - 2, t * P:(t + 1) * P], k.ident[:, :])
                    mm.then_inc(back, 1)

        @block.scalar
        def _(act):
            for c in range(NG):
                act.wait_ge(turned, c + 1)
                nc.scalar.activation(attnT[:, c, :], bank[:, c % 2, :], ACT.Copy).then_inc(taken, 1)

        @block.vector
        def _(dve):
            for c in range(NG + 1):
                if c < NG:
                    dve.wait_ge(projected, c + 1)
                    at = SEQ * b + c * CHUNK
                    nc.vector.tensor_tensor(product[:, c, :], bank[:, 2 + c % 2, :], gT[:, at:at + CHUNK], ALU.mult).then_inc(gated, 1)
                if c:
                    dve.wait_ge(back, c)
                    t0 = (b * NG + c - 1) * TPC
                    x = k.x[:, t0:t0 + TPC, :].rearrange("p t d -> p (t d)")
                    nc.vector.tensor_tensor(x, x, bank[:, 4 + (c - 1), :], ALU.add).then_inc(added, 1)

        @block.sync
        def _(sp):
            for c in range(NG):
                sp.wait_ge(added, c + 1)
                t0 = (b * NG + c) * TPC
                sp.dma_start(out_tiles[:, t0:t0 + TPC, :], k.x[:, t0:t0 + TPC, :]).then_inc(stored, 16)
            sp.wait_ge(stored, 16 * NG)


def build(nc, a, out):
    with ExitStack() as whole:
        def sb(ctx, name, shape, dt=F32):
            return ctx.enter_context(nc.sbuf_tensor(name, shape, dt))

        k, w = Core(), Core()
        k.nc = nc
        k.whole = whole
        k.bank = whole.enter_context(nc.psum_tensor("bank", [P, 8, CHUNK], F32))
        k.x = sb(whole, "x", [P, TILES, D])
        k.xnT = sb(whole, "xnT", [P, TOK])
        k.ident = sb(whole, "ident", [P, P])
        k.identb = sb(whole, "identb", [P, P], BF16)
        k.ones = sb(whole, "ones", [P, P])
        k.expert_rows = sb(whole, "expert_rows", [PARTS * EXPERTS, EXPERTS, P], BF16)
        k.sum_parity = sb(whole, "sum_parity", [P, 18])
        k.pair_mask = sb(whole, "pair_mask", [P, 2 * DK])
        k.weight_rank = sb(whole, "weight_rank", [P, EXPERTS])
        w.wqkv = sb(whole, "wqkv", [P, 3 * D])
        w.woT = sb(whole, "woT", [P, D])
        w.norm_w = sb(whole, "norm_w", [P, 2, DK])
        w.cos = sb(whole, "cos", [P, TPC, DK // 2])
        w.sin = sb(whole, "sin", [P, TPC, DK // 2])
        w.Wg1 = sb(whole, "Wg1", [P, EXPERTS])
        w.bg1 = sb(whole, "bg1", [P, EXPERTS])
        early = whole.enter_context(nc.semaphore("early_weights_in"))
        late = whole.enter_context(nc.semaphore("late_weights_in"))
        g1T = sb(whole, "g1T", [P, TOK])

        hidden0, hidden1 = a["L0_ffn_W1"].shape[2], a["L1_ffn_W1"].shape[2]
        n0, n1 = EXPERTS * hidden0 // P, EXPERTS * hidden1 // P
        second = ExitStack()
        W11 = sb(second, "W11", [P, EXPERTS * hidden1])
        W21 = sb(second, "W21", [P, n1, D])

        first = ExitStack()
        w.Wq, w.Wk, w.Wv = (sb(first, n, [P, D]) for n in ("Wq", "Wk", "Wv"))
        w.Wo = sb(first, "Wo", [P, 2, D])
        w.rw = sb(first, "rw", [P, HEADS * FEAT])
        w.bq, w.bk, w.bo = (sb(first, n, [P, 1]) for n in ("bq", "bk", "bo"))
        w.bv = sb(first, "bv", [P, D])
        Wg0 = sb(first, "Wg0", [P, EXPERTS])
        W10 = sb(first, "W10", [P, EXPERTS * hidden0])
        W20 = sb(first, "W20", [P, n0, D])
        b10 = sb(first, "b10", [P, n0])
        b20 = sb(first, "b20", [PARTS * EXPERTS, D])
        sT = sb(first, "sT", [P, TOK])

        column = lambda v: v.rearrange("(p o) -> p o", o=1)
        spread = lambda v: v.rearrange("(o n) -> o n", o=1).partition_broadcast(P)
        early_loads = [(w.Wq[:, :], a["L0_attn_Wq"]), (w.Wk[:, :], a["L0_attn_Wk"]), (w.Wv[:, :], a["L0_attn_Wv"]),
                       (w.bq[:, :], column(a["L0_attn_bq"])), (w.bk[:, :], column(a["L0_attn_bk"])),
                       (w.bo[:, :], column(a["L0_attn_bo"])), (w.bv[:, :], spread(a["L0_attn_bv"]))]
        early_loads += [(w.rw[DK * h:DK * (h + 1), FEAT * h:FEAT * (h + 1)], a["L0_attn_rw"][h]) for h in range(HEADS)]
        early_loads += [(w.Wo[32 * (j % 4):32 * (j % 4) + 2 * DK, j // 4, :], a["L0_attn_Wo"][2 * DK * j:2 * DK * (j + 1), :])
                        for j in range(PAIRS)]
        late_loads = [(Wg0[:, :], a["L0_ffn_Wg"]),
                      (W10[:, :].rearrange("p (e h) -> p e h", e=EXPERTS), a["L0_ffn_W1"].rearrange("e d h -> d e h")),
                      (W20[:, :, :], a["L0_ffn_W2"].rearrange("e (b p) d -> p (e b) d", p=P)),
                      (b10[:, :], a["L0_ffn_b1T"])]
        late_loads += [(b20[EXPERTS * i:EXPERTS * (i + 1), :], a["L0_ffn_b2"]) for i in range(PARTS)]
        late_loads += [(w.Wg1[:, :], a["L1_ffn_Wg"]), (w.bg1[:, :], spread(a["L1_ffn_bg"])),
                       (w.wqkv[:, 0:D], a["L1_attn_wqT"]), (w.wqkv[:, D:2 * D], a["L1_attn_wkT"]),
                       (w.wqkv[:, 2 * D:3 * D], a["L1_attn_wvT"]), (w.woT[:, :], a["L1_attn_woT"]),
                       (w.norm_w[:, 0, :], spread(a["L1_attn_q_norm_w"])), (w.norm_w[:, 1, :], spread(a["L1_attn_k_norm_w"])),
                       (W11[:, :].rearrange("p (e h) -> p e h", e=EXPERTS), a["L1_ffn_W1"].rearrange("e d h -> d e h")),
                       (W21[:, :, :], a["L1_ffn_W2"].rearrange("e (b p) d -> p (e b) d", p=P))]
        lead = TPC * P - ROPE
        for r, name in ((w.cos, "L1_attn_rope_cos"), (w.sin, "L1_attn_rope_sin")):
            late_loads += [(r[lead:P, 0, :], a[name][0:P - lead, :]),
                           (r[:, 1:TPC, :], a[name][P - lead:ROPE, :].rearrange("(t p) f -> p t f", p=P))]

        def load_weights(sp):
            for to, of in early_loads:
                sp.dma_start(to, of).then_inc(early, 16)
            for to, of in late_loads:
                sp.dma_start(to, of).then_inc(late, 16)

        k.load_weights = load_weights
        k.wait_weights = lambda eng: eng.wait_ge(early, 16 * len(early_loads))
        k.wait_late = lambda eng: eng.wait_ge(late, 16 * len(late_loads))
        k.clear = [(w.rw[:, :], 0.0), (w.Wo[:, :, :], 0.0), (w.cos[:, :, :], 1.0), (w.sin[:, :, :], 0.0)]

        constants(k)
        normalise(k, "ln0", a["L0_attn_x"])
        linear_attention(k, w, sT)
        with ExitStack() as ctx:
            gT = sb(ctx, "g0_parts", [PARTS * EXPERTS, TOK], BF16)
            gTf = sb(ctx, "g0_parts32", [PARTS * EXPERTS, TOK])
            gates(k, "gate0", Wg0, gT, gTf, top=2)
            experts(k, "ffn0", W10, W20, gT, hidden0, g1T, b10, b20, gTf)
        add_gated(k, sT, g1T)
        first.close()
        normalise(k, "ln1")
        with ExitStack() as ctx:
            gT = sb(ctx, "g1_parts", [PARTS * EXPERTS, TOK], BF16)
            gates(k, "gate1", w.Wg1, gT, None, w.bg1, top=1)
            experts(k, "ffn1", W11, W21, gT, hidden1, g1T)
        second.close()
        for b in range(BATCH):
            with ExitStack() as ctx:
                QT = sb(ctx, f"QT{b}", [P, PAIRS, SEQ], BF16)
                KT = sb(ctx, f"KT{b}", [P, PAIRS, SEQ], BF16)
                V = sb(ctx, f"V{b}", [P, SEQ // P, D])
                attn = sb(ctx, f"attn{b}", [P, SEQ // P, D])
                attention_operands(k, b, w, QT, KT, V)
                softmax_attention(k, b, QT, KT, V, attn)
                finish(k, b, w, attn, g1T, out)


_TURNED = {"L1_attn_wq": "L1_attn_wqT", "L1_attn_wk": "L1_attn_wkT", "L1_attn_wv": "L1_attn_wvT", "L1_attn_wo": "L1_attn_woT"}


def kernel(**inputs):
    import numpy as _np
    import concourse.bacc as _bacc
    from concourse import mybir as _mybir
    from concourse.bass_utils import run_bass_kernel_spmd as _run

    nc = _bacc.Bacc("TRN2", target_bir_lowering=False, num_devices=1)
    arrays, args = {}, {}
    for name, a in inputs.items():
        a = _np.asarray(a)
        if name in _TURNED:
            name, a = _TURNED[name], a.T
        elif name == "L0_ffn_b1":
            name, a = "L0_ffn_b1T", a.reshape(-1, P).T
        a = _np.ascontiguousarray(a)
        arrays[f"in_{name}_dram"] = a
        args[name] = nc.dram_tensor(f"in_{name}_dram", a.shape, _mybir.dt.from_np(a.dtype), kind="ExternalInput").ap()
    out = nc.dram_tensor("out_dram", (BATCH, SEQ, D), F32, kind="ExternalOutput").ap()
    build(nc, args, out)
    r = _run(nc, [arrays], core_ids=[0])
    return r.results[0]["out_dram"]
```

```python
from contextlib import ExitStack

import concourse.bass as bass
from concourse import mybir

F32 = mybir.dt.float32
BF16 = mybir.dt.bfloat16
ALU = mybir.AluOpType
ACT = mybir.ActivationFunctionType
X_AXIS = mybir.AxisListType.X

P = 128
BATCH, SEQ, D = 2, 2048, 128
TOK = BATCH * SEQ
TILES = TOK // P
CHUNK = 512
CHUNKS = TOK // CHUNK
TPC = CHUNK // P
HEADS = 16
DK = D // HEADS
PAIRS = HEADS // 2
FEAT = 64
EXPERTS = 8
LN_EPS = 1e-5
EPS = 1e-6
PARTS = 3
GROUPS = 4
GT = TILES // GROUPS
ROPE = 508
SLOT_TILES = TILES + EXPERTS - 1
SLOTS = SLOT_TILES * P

HEAD_ROWS = 64
SHIFT = 32


LOGIT = 0


class Core:
    pass


class Step:

    def __init__(self, turn, per_turn, number):
        self.turn, self.per_turn, self.number = turn, per_turn, number

    def __add__(self, n):
        return Step(self.turn, self.per_turn, self.number + n)

    def at(self, each, more):
        constant = self.number * each + more
        return constant if self.turn is None else self.turn * (self.per_turn * each) + constant


def bc(ap, shape):
    return ap.to_broadcast(shape)


def stage_semaphores(k, ctx, stage, again=False):
    nc, taken = k.nc, []
    if not again:
        return lambda name: k.whole.enter_context(nc.semaphore(stage + name))

    def clear(failed, *_):
        if failed:
            return
        with nc.Block() as block:
            @block.gpsimd
            def _(pool):
                for semaphore in taken:
                    pool.sem_clear(semaphore)

    def sem(name):
        taken.append(ctx.enter_context(nc.semaphore(stage + name)))
        return taken[-1]

    ctx.push(clear)
    return sem


def constants(k, pool):
    cleared = k.cleared
    for ap, value in k.clear:
        pool.memset(ap, value).then_inc(k.rw_cleared, 1)
    pool.memset(k.ident[:, :], 0.0).then_inc(cleared, 1)
    pool.memset(k.identb[:, :], 0.0).then_inc(cleared, 1)
    pool.memset(k.expert_rows[:, :, :], 0.0).then_inc(cleared, 1)
    pool.memset(k.ones[:, :], 1.0)
    pool.memset(k.before[:, :], 1.0).then_inc(cleared, 1)
    pool.memset(k.zeros[:, :], 0.0).then_inc(k.zeros_ready, 1)
    pool.iota(k.number[:, :], [[1, SLOT_TILES]], base=0, channel_multiplier=0, allow_small_or_imprecise_dtypes=True)
    pool.iota(k.tile_start[:, :], [[P, TILES]], base=0, channel_multiplier=0, allow_small_or_imprecise_dtypes=True)
    pool.memset(k.sum_parity[:, :], 0.0).then_inc(cleared, 1)
    pool.memset(k.pair_mask[:, :], 0.0).then_inc(cleared, 1)
    pool.memset(k.weight_rank[:, :], 0.0).then_inc(cleared, 1)
    n = 7
    pool.wait_ge(cleared, n)
    pool.affine_select(out=k.before[:, :], in_=k.before[:, :], compare_op=ALU.is_ge, fill=0.0, base=-1,
                       pattern=[[1, P]], channel_multiplier=-1)
    for m in (k.ident, k.identb):
        pool.affine_select(out=m[:, :], in_=m[:, :], compare_op=ALU.not_equal, fill=1.0, base=0,
                           pattern=[[-1, P]], channel_multiplier=1).then_inc(cleared, 1)
    n += 2
    for part in range(PARTS):
        pool.affine_select(out=k.expert_rows[:, :, :], in_=k.expert_rows[:, :, :],
                           compare_op=ALU.not_equal, fill=1.0, base=-EXPERTS * part,
                           pattern=[[-1, EXPERTS], [0, P]], channel_multiplier=1).then_inc(cleared, 1)
        n += 1
        pool.wait_ge(cleared, n)
    for group in range(4):
        head = group % 2
        cols = k.sum_parity[:, 9 * head:9 * head + 9]
        pool.affine_select(out=cols, in_=cols, compare_op=ALU.not_equal, fill=1.0, base=-32 * group,
                           pattern=[[-1, 9]], channel_multiplier=1).then_inc(cleared, 1)
        n += 1
        pool.wait_ge(cleared, n)
    pool.memset(k.pair_mask[0:FEAT, 0:DK], 1.0).then_inc(cleared, 1)
    pool.wait_ge(cleared, n + 1)
    pool.memset(k.pair_mask[FEAT:P, DK:2 * DK], 1.0).then_inc(cleared, 1)
    pool.wait_ge(cleared, n + 2)
    for e in range(EXPERTS):
        pool.memset(k.weight_rank[:, e:e + 1], float(EXPERTS - e))
    k.identities_cleared = n + 2


def normalise(k, tag, Wg, wait_gate, rows=None, load=None, x_dram=None):
    nc = k.nc
    x, xnT, bank = k.x, k.xnT, k.bank
    with ExitStack() as ctx:
        sem = stage_semaphores(k, ctx, f"{tag}_")
        xc = ctx.enter_context(nc.sbuf_tensor(f"{tag}_centred", [P, TILES, D], F32))
        sq = rows if rows is not None else ctx.enter_context(nc.sbuf_tensor(f"{tag}_squares", [P, TILES, D], F32))
        st = ctx.enter_context(nc.sbuf_tensor(f"{tag}_stats", [P, 5, TILES], F32))
        total, mean, var, root, rstd = (st[:, i, :] for i in range(5))
        summed, centred, squared, varred, rooted, scaled, normed, turned, evacuated = (
            sem(n) for n in ("summed", "centred", "squared", "varred", "rooted", "scaled", "normed",
                             "turned", "evacuated"))
        block = ctx.enter_context(nc.Block())

        def tiles(g):
            return slice(g * GT, (g + 1) * GT)

        if load is not None:

            @block.sync
            def _(sp):
                if x_dram is not None:
                    k.load_gate(sp)
                    x_tiles = x_dram.rearrange("b (t p) d -> p (b t) d", p=P)
                    for g in range(GROUPS):
                        sp.dma_start(x[:, tiles(g), :], x_tiles[:, tiles(g), :]).then_inc(k.x_in[g], 16)
                load(sp)

        @block.vector
        def _(dve):
            def centre(g):
                if x_dram is not None:
                    dve.wait_ge(k.x_in[g], 16)
                nc.vector.tensor_reduce(total[:, tiles(g)], x[:, tiles(g), :], X_AXIS, ALU.add).then_inc(summed, 1)
                dve.wait_ge(summed, 2 * g + 1)
                nc.vector.tensor_scalar(mean[:, tiles(g)], total[:, tiles(g)], 1.0 / D, None, ALU.mult).then_inc(summed, 1)
                dve.wait_ge(summed, 2 * g + 2)
                nc.vector.tensor_tensor(xc[:, tiles(g), :], x[:, tiles(g), :],
                                        bc(mean[:, tiles(g)].unsqueeze(2), [P, GT, D]), ALU.subtract).then_inc(centred, 1)

            def variance(g):
                dve.wait_ge(squared, g + 1)
                nc.vector.tensor_reduce(total[:, tiles(g)], sq[:, tiles(g), :], X_AXIS, ALU.add).then_inc(varred, 1)
                dve.wait_ge(varred, 2 * g + 1)
                nc.vector.tensor_scalar(var[:, tiles(g)], total[:, tiles(g)], 1.0 / D, LN_EPS, ALU.mult, ALU.add).then_inc(varred, 1)
                dve.wait_ge(rooted, g + 1)
                nc.vector.reciprocal(rstd[:, tiles(g)], root[:, tiles(g)]).then_inc(scaled, 1)

            centre(0)
            for g in range(GROUPS):
                if g + 1 < GROUPS:
                    centre(g + 1)
                variance(g)

        @block.gpsimd
        def _(pool):
            if x_dram is not None:
                constants(k, pool)
            for g in range(GROUPS):
                pool.wait_ge(scaled, g + 1)
                nc.gpsimd.tensor_tensor(sq[:, tiles(g), :], xc[:, tiles(g), :],
                                        bc(rstd[:, tiles(g)].unsqueeze(2), [P, GT, D]), ALU.mult).then_inc(normed, 1)

        @block.scalar
        def _(act):
            def square(g):
                act.wait_ge(centred, g + 1)
                nc.scalar.activation(sq[:, tiles(g), :], xc[:, tiles(g), :], ACT.Square).then_inc(squared, 1)

            def evacuate(g):
                for c in (2 * g, 2 * g + 1):
                    act.wait_ge(turned, c + 1)
                    nc.scalar.activation(xnT[:, c * CHUNK:(c + 1) * CHUNK], bank[:, 1 + c % 7, :], ACT.Copy).then_inc(evacuated, 1)

            square(0)
            for g in range(GROUPS):
                if g + 1 < GROUPS:
                    square(g + 1)
                act.wait_ge(varred, 2 * g + 2)
                nc.scalar.activation(root[:, tiles(g)], var[:, tiles(g)], ACT.Sqrt).then_inc(rooted, 1)
                if g:
                    evacuate(g - 1)
            evacuate(GROUPS - 1)

        @block.tensor
        def _(pe):
            if x_dram is not None:
                pe.wait_ge(k.cleared, k.identities_cleared)
            for g in range(GROUPS):
                pe.wait_ge(normed, g + 1)
                for c in (2 * g, 2 * g + 1):
                    if c >= 7:
                        pe.wait_ge(evacuated, c - 6)
                    for t in range(TPC):
                        mm = nc.tensor.transpose(bank[:, 1 + c % 7, t * P:(t + 1) * P], sq[:, c * TPC + t, :], k.ident[:, :])
                    mm.then_inc(turned, 1)
                if g == 0:
                    wait_gate(pe)
                for c in (2 * g, 2 * g + 1):
                    pe.wait_ge(evacuated, c + 1)
                    for t in range(c * TPC, (c + 1) * TPC):
                        nc.tensor.matmul(bank[:, LOGIT, t * EXPERTS:(t + 1) * EXPERTS], xnT[:, t * P:(t + 1) * P], Wg[:, :],
                                         start=True, stop=True)


def linear_attention(k, w, sT):
    nc = k.nc
    xnT, bank = k.xnT, k.bank
    FR = 8
    with ExitStack() as ctx:
        sem = stage_semaphores(k, ctx, "la_")
        sb = lambda name, shape: ctx.enter_context(nc.sbuf_tensor(f"la_{name}", shape, F32))
        qT = sb("qT", [P, TOK])
        kT = sb("kT", [P, SEQ])
        v = sb("v", [P, TILES // BATCH, PAIRS, 32])
        feat = sb("feat", [P, FR, CHUNK])
        kvT = sb("kvT", [P, 2, P])
        num_w = sb("num_w", [P, PAIRS, 32])
        den_w = sb("den_w", [P, PAIRS, 32])
        den = sb("den", [P, 2, CHUNK])
        eps = sb("eps", [P, 1])
        outT = sb("outT", [P, 4, CHUNK])
        (cleared, q_ready, k_ready, v_ready, q_out, k_out, v_out, feat_ready, feat_out, feat_used,
         kv_out, kvT_ready, weights_out, relu_out, eps_out, den_out, den_step, out_ready, s_ready, s_out) = (
            sem(n) for n in ("cleared", "q_ready", "k_ready", "v_ready", "q_out", "k_out", "v_out", "feat_ready",
                             "feat_out", "feat_used", "kv_out", "kvT_ready", "weights_out",
                             "relu_out", "eps_out", "den_out", "den_step", "out_ready", "s_ready", "s_out"))
        block = ctx.enter_context(nc.Block())
        CB = CHUNKS // BATCH
        NF = 2 * TPC * CB
        Q_BANK, K_BANK, V_BANK, F_BANK, KV_BANK, T_BANK = 0, 1, 2, 3, 5, 7
        NUM_BANK, DEN_BANK, S_BANK = (0, 2), (1, 7), 5

        def group_of(b, g):
            return 2 * CB * b + g


        @block.gpsimd
        def _(pool):
            pool.memset(v[:, :, :, 2 * DK + 1:32], 0.0).then_inc(cleared, 1)
            pool.memset(v[:, :, :, 2 * DK:2 * DK + 1], 1.0).then_inc(cleared, 1)
            pool.memset(num_w[:, :, :], 0.0).then_inc(cleared, 1)
            pool.memset(den_w[:, :, :], 0.0).then_inc(cleared, 1)
            pool.memset(eps[:, :], EPS).then_inc(cleared, 1)

        @block.tensor
        def _(pe):
            k.wait_weights(pe)

            def project(b, c):
                if b > 0 or c > 0:
                    pe.wait_ge(q_out, CB * b + c)
                    pe.wait_ge(k_out, CB * b + c)
                    pe.wait_ge(v_out, CB * b + c)
                at = (CB * b + c) * CHUNK
                nc.tensor.matmul(bank[:, Q_BANK, :], w.Wq[:, :], xnT[:, at:at + CHUNK], start=True, stop=True).then_inc(q_ready, 1)
                nc.tensor.matmul(bank[:, K_BANK, :], w.Wk[:, :], xnT[:, at:at + CHUNK], start=True, stop=True).then_inc(k_ready, 1)
                for t in range(TPC):
                    mm = nc.tensor.matmul(bank[:, V_BANK, t * P:(t + 1) * P], xnT[:, at + t * P:at + (t + 1) * P],
                                          w.Wv[:, :], start=True, stop=True)
                mm.then_inc(v_ready, 1)

            def feature(f, lhsT, rhs):
                if f >= 2:
                    last_b, last = (f - 2) // (2 * NF), (f - 2) % (2 * NF)
                    if last >= NF:
                        pe.wait_ge(relu_out, NF * last_b + last - NF + 1)
                    else:
                        pe.wait_ge(feat_out, NF * last_b + last + 1)
                nc.tensor.matmul(bank[:, F_BANK + f % 2, :], lhsT, rhs, start=True, stop=True).then_inc(feat_ready, 1)

            def keys_values(b, i):
                f = 2 * NF * b + i
                tile, half = i // 2, i % 2
                pe.wait_ge(feat_out, NF * b + i + 1)
                pe.wait_ge(v_out, CB * b + tile // TPC + 1)
                for j in range(4):
                    mm = nc.tensor.matmul(bank[32 * j:32 * j + 32, KV_BANK + half, 0:P], v[:, tile, 4 * half + j, :],
                                          feat[:, f % FR, j * P:(j + 1) * P], start=(tile == 0),
                                          stop=(tile == TILES // BATCH - 1), tile_position=(0, 32 * j))
                mm.then_inc(feat_used, 1)
                return mm

            def quotient(b, g):
                n = group_of(b, g)
                f0 = 2 * NF * b + NF + 4 * g
                pe.wait_ge(eps_out, n + 1)
                if n >= 2:
                    pe.wait_ge(out_ready, n - 1)
                for weight, to in ((num_w, NUM_BANK[g % 2]), (den_w, DEN_BANK[g % 2])):
                    for j in range(4):
                        mm = nc.tensor.matmul(bank[32 * j:32 * j + 32, to, :], weight[:, 4 * (g % 2) + j, :],
                                              feat[:, (f0 + j) % FR, :], start=True, stop=True,
                                              tile_position=(0, 32 * j))
                mm.then_inc(feat_used, 4)

            def project_out(b, c):
                n = CB * b + c
                pe.wait_ge(out_ready, 2 * n + 2)
                if n >= 2:
                    pe.wait_ge(s_out, n - 1)
                for half in range(2):
                    mm = nc.tensor.matmul(bank[:, S_BANK + n % 2, :], w.Wo[:, half, :], outT[:, (2 * n + half) % 4, :],
                                          start=(half == 0), stop=(half == 1))
                mm.then_inc(s_ready, 1)

            for b in range(BATCH):
                if b == 0:
                    project(0, 0)
                    pe.wait_ge(cleared, 5)
                if b > 0:
                    pe.wait_ge(out_ready, group_of(b, 0))
                    pe.wait_ge(s_out, CB * b)
                for i in range(NF):
                    if i % (2 * TPC) == 0:
                        if b > 0 or i > 0:
                            project(b, i // (2 * TPC))
                        pe.wait_ge(k_out, CB * b + i // (2 * TPC) + 1)
                    at = (i // 2) * P
                    feature(2 * NF * b + i, kT[:, at:at + P], w.rw[:, (i % 2) * CHUNK:(i % 2 + 1) * CHUNK])
                    if i:
                        keys_values(b, i - 1)
                keys_values(b, NF - 1)
                pe.wait_ge(kv_out, b + 1)
                for half in range(2):
                    mm = nc.tensor.transpose(bank[:, T_BANK, half * P:(half + 1) * P], kvT[:, half, :], k.ident[:, :])
                mm.then_inc(kvT_ready, 1)
                pe.wait_ge(q_out, CB * (b + 1))
                pe.wait_ge(weights_out, 2 * (b + 1))
                for g in range(2 * CB):
                    at = SEQ * b + (g // 2) * CHUNK
                    for j in range(4):
                        pair = 4 * (g % 2) + j
                        feature(2 * NF * b + NF + 4 * g + j, w.rw[:, pair * P:(pair + 1) * P], qT[:, at:at + CHUNK])
                    if g >= 1:
                        quotient(b, g - 1)
                    if g % 2 and g >= 3:
                        project_out(b, (g - 3) // 2)
                quotient(b, 2 * CB - 1)
                project_out(b, CB - 1)

        @block.scalar
        def _(act):
            k.wait_weights(act)
            act.wait_ge(cleared, 5)

            def relu(b, q):
                f = 2 * NF * b + NF + q
                act.wait_ge(feat_ready, f + 1)
                act.wait_ge(feat_used, f - FR + 1)
                nc.scalar.activation(feat[:, f % FR, :], bank[:, F_BANK + f % 2, :], ACT.Relu).then_inc(relu_out, 1)

            def denominators(b, g):
                n = group_of(b, g)
                act.wait_ge(feat_used, 2 * NF * b + NF + 4 * (g + 1))
                if n >= 2:
                    act.wait_ge(out_ready, n - 1)
                nc.scalar.activation(den[:, n % 2, :], bank[:, DEN_BANK[g % 2], :], ACT.Identity, bias=eps[:, :]).then_inc(den_out, 1)

            def keep(b, c):
                n = CB * b + c
                act.wait_ge(s_ready, n + 1)
                nc.scalar.activation(sT[:, n * CHUNK:(n + 1) * CHUNK], bank[:, S_BANK + n % 2, :], ACT.Identity,
                                     bias=w.bo[:, :]).then_inc(s_out, 1)

            for b in range(BATCH):
                for c in range(CB):
                    n = CB * b + c
                    act.wait_ge(q_ready, n + 1)
                    nc.scalar.activation(qT[:, n * CHUNK:(n + 1) * CHUNK], bank[:, Q_BANK, :], ACT.Identity,
                                         bias=w.bq[:, :]).then_inc(q_out, 1)
                    act.wait_ge(k_ready, n + 1)
                    nc.scalar.activation(kT[:, c * CHUNK:(c + 1) * CHUNK], bank[:, K_BANK, :], ACT.Identity,
                                         bias=w.bk[:, :]).then_inc(k_out, 1)
                act.wait_ge(feat_used, 2 * NF * b + NF)
                nc.scalar.activation(kvT[:, :, :], bank[:, KV_BANK:KV_BANK + 2, 0:P], ACT.Copy).then_inc(kv_out, 1)
                for g in range(2 * CB + 1):
                    if g < 2 * CB:
                        for j in range(4):
                            relu(b, 4 * g + j)
                    if g:
                        denominators(b, g - 1)
                    if g % 2 and g >= 3:
                        keep(b, (g - 3) // 2)
                keep(b, CB - 1)

        @block.vector
        def _(dve):
            k.wait_weights(dve)
            dve.wait_ge(cleared, 5)

            def feature(f):
                dve.wait_ge(feat_ready, f + 1)
                if f >= FR:
                    dve.wait_ge(feat_used, f - FR + 1)
                nc.vector.tensor_scalar(feat[:, f % FR, :], bank[:, F_BANK + f % 2, :], 0.0, EPS, ALU.max, ALU.add).then_inc(feat_out, 1)

            def divide(b, g):
                n = group_of(b, g)
                slot = den[:, n % 2, :]
                dve.wait_ge(den_out, n + 1)
                nc.vector.reciprocal(slot, slot).then_inc(den_step, 1)
                dve.wait_ge(den_step, n + 1)
                if n >= 4:
                    dve.wait_ge(s_ready, (n - 4) // 2 + 1)
                nc.vector.tensor_tensor(outT[:, n % 4, :], bank[:, NUM_BANK[g % 2], :], slot, ALU.mult).then_inc(out_ready, 1)

            for b in range(BATCH):
                for i in range(NF):
                    if i % (2 * TPC) == 0:
                        c = i // (2 * TPC)
                        dve.wait_ge(v_ready, CB * b + c + 1)
                        nc.vector.tensor_tensor(v[:, c * TPC:(c + 1) * TPC, :, 0:2 * DK],
                                                bank[:, V_BANK, :].rearrange("p (t j e) -> p t j e", t=TPC, j=PAIRS),
                                                bc(w.bv[:, :].rearrange("p (j e) -> p j e", j=PAIRS).unsqueeze(1), [P, TPC, PAIRS, 2 * DK]),
                                                ALU.add).then_inc(v_out, 1)
                    feature(2 * NF * b + i)
                dve.wait_ge(kvT_ready, b + 1)
                turned = bank[:, T_BANK, 0:2 * P].rearrange("p (j e) -> p j e", e=32)
                mask = bc(k.pair_mask[:, :].unsqueeze(1), [P, PAIRS, 2 * DK])
                nc.vector.tensor_tensor(num_w[:, :, 0:2 * DK], turned[:, :, 0:2 * DK], mask, ALU.mult).then_inc(weights_out, 1)
                nc.vector.tensor_tensor(den_w[:, :, 0:2 * DK], bc(turned[:, :, 2 * DK:2 * DK + 1], [P, PAIRS, 2 * DK]), mask, ALU.mult).then_inc(weights_out, 1)
                for g in range(2 * CB + 1):
                    if g < 2 * CB:
                        at = (2 * NF * b + NF + 4 * g) % FR
                        dve.wait_ge(relu_out, NF * b + 4 * g + 4)
                        nc.vector.tensor_scalar(feat[:, at:at + 4, :], feat[:, at:at + 4, :], EPS, None, ALU.add).then_inc(eps_out, 1)
                    if g:
                        divide(b, g - 1)


def gates(k, tag, gT, gTf):
    nc = k.nc
    bank, xnT = k.bank, k.xnT
    with ExitStack() as ctx:
        sem = stage_semaphores(k, ctx, f"{tag}_")
        sb = lambda name, shape, dt=F32: ctx.enter_context(nc.sbuf_tensor(f"{tag}_{name}", shape, dt))
        p = sb("probs", [P, TILES, EXPERTS])
        left = sb("left", [P, TILES, EXPERTS])
        hot = sb("hot", [P, TILES, EXPERTS])
        mask = sb("mask", [P, TILES, EXPERTS])
        one = sb("one", [P, TILES])
        parts = sb("parts", [P, TILES, PARTS * EXPERTS], BF16)
        stepped, exped, exp_ready, gates_ready, turned, taken = (
            sem(n) for n in ("stepped", "exped", "exp_ready", "gates_ready",
                             "turned", "taken"))
        block = ctx.enter_context(nc.Block())
        wide = [P, TILES, EXPERTS]
        TURN = 2
        TOP = 2
        per = 1024 // P

        @block.tensor
        def _(pe):
            pe.wait_ge(gates_ready, 1)
            for t in range(TILES):
                out = bank[:, TURN + t // per, :].bitcast(BF16)[0:PARTS * EXPERTS, (t % per) * P:(t % per + 1) * P]
                mm = nc.tensor.transpose(out, parts[:, t, :], k.identb[:, :])
                if t % per == per - 1:
                    mm.then_inc(turned, 1)

        @block.scalar
        def _(act):
            act.wait_ge(exp_ready, 1)
            nc.scalar.activation(p[:, :, :], left[:, :, :], ACT.Exp).then_inc(exped, 1)
            for n in range(TILES // per):
                act.wait_ge(turned, n + 1)
                src = bank[:, TURN + n, :].bitcast(BF16)[0:PARTS * EXPERTS, :]
                nc.scalar.activation(gT[:, n * per * P:(n + 1) * per * P], src, ACT.Copy).then_inc(taken, 1)
                nc.scalar.activation(gTf[:, n * per * P:(n + 1) * per * P], src, ACT.Copy).then_inc(taken, 1)

        @block.vector
        def _(dve):
            n = 0

            def step(ins):
                nonlocal n
                ins.then_inc(stepped, 1)
                n += 1
                dve.wait_ge(stepped, n)

            tt, red = nc.vector.tensor_tensor, nc.vector.tensor_reduce
            spread = lambda a: bc(a.unsqueeze(2), wide)
            logits = bank[:, LOGIT, 0:TILES * EXPERTS].rearrange("p (t e) -> p t e", e=EXPERTS)
            step(red(one[:, :], logits, X_AXIS, ALU.max))
            tt(left[:, :, :], logits, spread(one[:, :]), ALU.subtract).then_inc(exp_ready, 1)
            dve.wait_ge(exped, 1)
            step(red(one[:, :], p[:, :, :], X_AXIS, ALU.add))
            step(nc.vector.reciprocal(one[:, :], one[:, :]))
            step(tt(p[:, :, :], p[:, :, :], spread(one[:, :]), ALU.mult))
            step(nc.vector.tensor_copy(left[:, :, :], p[:, :, :]))
            for turn in range(TOP):
                step(red(one[:, :], left[:, :, :], X_AXIS, ALU.max))
                step(tt(hot[:, :, :], left[:, :, :], spread(one[:, :]), ALU.is_equal))
                step(tt(hot[:, :, :], hot[:, :, :], bc(k.weight_rank[:, :].unsqueeze(1), wide), ALU.mult))
                step(red(one[:, :], hot[:, :, :], X_AXIS, ALU.max))
                step(tt(hot[:, :, :], hot[:, :, :], spread(one[:, :]), ALU.is_equal))
                if turn == 0:
                    step(nc.vector.tensor_copy(mask[:, :, :], hot[:, :, :]))
                else:
                    step(tt(mask[:, :, :], mask[:, :, :], hot[:, :, :], ALU.add))
                if turn + 1 < TOP:
                    step(nc.vector.scalar_tensor_tensor(left[:, :, :], hot[:, :, :], -2.0, left[:, :, :], ALU.mult, ALU.add))
            step(tt(p[:, :, :], p[:, :, :], mask[:, :, :], ALU.mult))
            part = lambda i: parts[:, :, i * EXPERTS:(i + 1) * EXPERTS]
            step(nc.vector.tensor_copy(part(0), p[:, :, :]))
            step(tt(left[:, :, :], p[:, :, :], part(0), ALU.subtract))
            step(nc.vector.tensor_copy(part(1), left[:, :, :]))
            tt(part(2), left[:, :, :], part(1), ALU.subtract).then_inc(gates_ready, 1)


def route(k, tag, bg, rows, r, sorted_dram):
    nc = k.nc
    bank, xnT = k.bank, k.xnT
    with ExitStack() as ctx:
        sem = stage_semaphores(k, ctx, f"{tag}_")
        sb = lambda name, shape, dt=F32: ctx.enter_context(nc.sbuf_tensor(f"{tag}_{name}", shape, dt))
        p = sb("probs", [P, TILES, EXPERTS])
        left = sb("left", [P, TILES, EXPERTS])
        hot = sb("hot", [P, TILES, EXPERTS])
        counts = [sb(f"counts{i}", [P, TILES, EXPERTS]) for i in range(2)]
        over = sb("over", [P, EXPERTS, TILES])
        upto = sb("upto", [P, EXPERTS, EXPERTS])
        tiles = sb("tiles", [P, 3, EXPERTS])
        past = sb("past", [P, SLOT_TILES, EXPERTS])
        at = sb("at", [P, SLOT_TILES])
        one = sb("one", [P, TILES])
        col = sb("col", [P, EXPERTS])
        stepped, exped, exp_ready, sum_ready, sum_done, hot_ready, counted, slot_ready, scattered = (
            sem(n) for n in ("stepped", "exped", "exp_ready", "sum_ready", "sum_done", "hot_ready",
                             "counted", "slot_ready", "scattered"))
        block = ctx.enter_context(nc.Block())
        wide = [P, TILES, EXPERTS]
        SUM, WITHIN, TOTAL = 1, 2, 3
        NW = TILES * EXPERTS

        @block.tensor
        def _(pe):
            pe.wait_ge(hot_ready, 1)
            flat = hot[:, :, :].rearrange("p t e -> p (t e)")
            nc.tensor.matmul(bank[:, WITHIN, 0:NW], k.before[:, :], flat, start=True, stop=True)
            nc.tensor.matmul(bank[:, TOTAL, 0:NW], k.ones[:, :], flat, start=True, stop=True).then_inc(counted, 1)
            pe.wait_ge(sum_ready, 1)
            nc.tensor.matmul(bank[:, SUM, 0:EXPERTS], k.ones[:, :], col[:, :], start=True, stop=True).then_inc(sum_done, 1)

        @block.scalar
        def _(act):
            act.wait_ge(exp_ready, 1)
            nc.scalar.activation(p[:, :, :], left[:, :, :], ACT.Exp).then_inc(exped, 1)

        @block.gpsimd
        def _(pool):
            pool.wait_ge(k.zeros_stored, 16 * 8)
            pool.wait_ge(slot_ready, 1)
            for t in range(TILES):
                pool.indirect_dma_start(sorted_dram, bass.IndirectOffsetOnAxis(ap=r.slot[:, t:t + 1], axis=0),
                                        rows[:, t, :], None).then_inc(scattered, 16)
            pool.wait_ge(scattered, 16 * TILES)


        @block.vector
        def _(dve):
            n = 0

            def step(ins):
                nonlocal n
                ins.then_inc(stepped, 1)
                n += 1
                dve.wait_ge(stepped, n)

            tt, ts, red, cp = nc.vector.tensor_tensor, nc.vector.tensor_scalar, nc.vector.tensor_reduce, nc.vector.tensor_copy
            spread = lambda a: bc(a.unsqueeze(2), wide)
            in_bank = lambda i: bank[:, i, 0:NW].rearrange("p (t e) -> p t e", e=EXPERTS)
            number = k.number[:, 0:EXPERTS]
            tt(upto[:, :, :], bc(number.unsqueeze(2), [P, EXPERTS, EXPERTS]), bc(number.unsqueeze(1), [P, EXPERTS, EXPERTS]), ALU.is_ge)
            step(tt(p[:, :, :], in_bank(LOGIT), bc(bg[:, :].unsqueeze(1), wide), ALU.add))
            step(red(one[:, :], p[:, :, :], X_AXIS, ALU.max))
            tt(left[:, :, :], p[:, :, :], spread(one[:, :]), ALU.subtract).then_inc(exp_ready, 1)
            dve.wait_ge(exped, 1)
            step(red(one[:, :], p[:, :, :], X_AXIS, ALU.add))
            step(nc.vector.reciprocal(one[:, :], one[:, :]))
            step(tt(p[:, :, :], p[:, :, :], spread(one[:, :]), ALU.mult))
            step(red(one[:, :], p[:, :, :], X_AXIS, ALU.max))
            step(tt(hot[:, :, :], p[:, :, :], spread(one[:, :]), ALU.is_equal))
            step(tt(hot[:, :, :], hot[:, :, :], bc(k.weight_rank[:, :].unsqueeze(1), wide), ALU.mult))
            step(red(one[:, :], hot[:, :, :], X_AXIS, ALU.max))
            tt(hot[:, :, :], hot[:, :, :], spread(one[:, :]), ALU.is_equal).then_inc(hot_ready, 1)
            dve.wait_ge(counted, 1)
            step(cp(counts[0][:, :, :], in_bank(TOTAL)))
            i, d = 0, 1
            while d < TILES:
                cp(counts[1 - i][:, 0:d, :], counts[i][:, 0:d, :])
                step(tt(counts[1 - i][:, d:TILES, :], counts[i][:, d:TILES, :], counts[i][:, 0:TILES - d, :], ALU.add))
                i, d = 1 - i, 2 * d
            total = counts[i][:, TILES - 1, :]
            mine, end, start = (tiles[:, j, :] for j in range(3))
            step(tt(over[:, :, :], bc(total.unsqueeze(2), [P, EXPERTS, TILES]), bc(k.tile_start[:, :].unsqueeze(1), [P, EXPERTS, TILES]), ALU.is_gt))
            step(red(mine, over[:, :, :], X_AXIS, ALU.add))
            step(tt(upto[:, :, :], upto[:, :, :], bc(mine.unsqueeze(1), [P, EXPERTS, EXPERTS]), ALU.mult))
            step(red(end, upto[:, :, :], X_AXIS, ALU.add))
            step(tt(start, end, mine, ALU.subtract))
            step(ts(start, start, float(P), None, ALU.mult))
            step(tt(left[:, :, :], counts[i][:, :, :], bc(start.unsqueeze(1), wide), ALU.add))
            step(tt(left[:, :, :], left[:, :, :], in_bank(TOTAL), ALU.subtract))
            step(tt(left[:, :, :], left[:, :, :], in_bank(WITHIN), ALU.add))
            step(tt(left[:, :, :], left[:, :, :], hot[:, :, :], ALU.mult))
            step(red(one[:, :], left[:, :, :], X_AXIS, ALU.add))
            cp(r.slot[:, :], one[:, :]).then_inc(slot_ready, 1)
            step(tt(past[:, :, :], bc(k.number[:, :].unsqueeze(2), [P, SLOT_TILES, EXPERTS]), bc(end.unsqueeze(1), [P, SLOT_TILES, EXPERTS]), ALU.is_ge))
            step(red(at[:, :], past[:, :, :], X_AXIS, ALU.add))
            step(ts(at[:, :], at[:, :], float(EXPERTS - 1), float(r.hidden), ALU.min, ALU.mult))
            cp(r.weight_at[:, :], at[:, :])
            step(tt(p[:, :, :], p[:, :, :], hot[:, :, :], ALU.mult))
            red(col[:, :], p[:, :, :].rearrange("p t e -> p e t"), X_AXIS, ALU.add).then_inc(sum_ready, 1)
            dve.wait_ge(sum_done, 1)
            step(ts(col[:, :], bank[:, SUM, 0:EXPERTS], EPS, None, ALU.add))
            step(nc.vector.reciprocal(col[:, :], col[:, :]))
            step(tt(p[:, :, :], p[:, :, :], bc(col[:, :].unsqueeze(1), wide), ALU.mult))
            step(ts(p[:, :, :], p[:, :, :], float(TOK), None, ALU.mult))
            red(r.gate[:, :], p[:, :, :], X_AXIS, ALU.add)


def sorted_experts(k, tag, W1, W2, r, sorted_dram, made_dram):
    nc = k.nc
    bank = k.bank
    HB = r.hidden // P
    GROUP_OF = 13
    NG = SLOT_TILES // GROUP_OF
    R = 3
    TURNS = SLOT_TILES // R
    assert NG * GROUP_OF == SLOT_TILES and TURNS * R == SLOT_TILES
    with ExitStack() as ctx:
        sem = stage_semaphores(k, ctx, f"{tag}_")
        sb = lambda name, shape, dt=F32: ctx.enter_context(nc.sbuf_tensor(f"{tag}_{name}", shape, dt))
        slots = sb("slots", [P, SLOT_TILES, D])
        slotsT = sb("slotsT", [P, SLOTS])
        w1 = sb("w1", [P, R, r.hidden])
        w2 = sb("w2", [P, R, HB * D])
        hT = sb("hT", [P, R, HB * P])
        x_in = [sem(f"x_in{g}") for g in range(NG)]
        (cleared, x_turned, xT_out, copy_allowed, w1_ready, w2_ready, h_ready, h_out, y_ready, y_out) = (
            sem(n) for n in ("cleared", "x_turned", "xT_out", "copy_allowed", "w1_ready", "w2_ready", "h_ready", "h_out", "y_ready",
                             "y_out"))
        block = ctx.enter_context(nc.Block())
        H_BANK, Y_BANK, T_BANK = 0, R, 2 * R
        T_BANKS = 8 - T_BANK
        NT = -(-SLOT_TILES // TPC)
        FREE = R
        dram_tiles = lambda d, g: d[g * GROUP_OF * P:(g + 1) * GROUP_OF * P, :].rearrange("(j p) d -> p j d", p=P)
        group = lambda g: slots[:, g * GROUP_OF:(g + 1) * GROUP_OF, :]
        in_bank = lambda n: min(TPC, SLOT_TILES - n * TPC)

        @block.sync
        def _(sp):
            for g in range(NG):
                sp.dma_start(group(g), dram_tiles(sorted_dram, g)).then_inc(x_in[g], 16)
            for g in range(NG):
                sp.wait_ge(y_out, (g + 1) * GROUP_OF + FREE)
                sp.dma_start(dram_tiles(made_dram, g), group(g)).then_inc(k.made_stored, 16)
            sp.wait_ge(k.made_stored, 16 * NG)

        @block.tensor
        def _(pe):
            for n in range(NT):
                if n >= T_BANKS:
                    pe.wait_ge(xT_out, n - T_BANKS + 1)
                pe.wait_ge(x_in[(n * TPC + in_bank(n) - 1) // GROUP_OF], 16)
                for i in range(in_bank(n)):
                    mm = nc.tensor.transpose(bank[:, T_BANK + n % T_BANKS, i * P:(i + 1) * P], slots[:, n * TPC + i, :], k.ident[:, :])
                mm.then_inc(x_turned, 1)

            def hidden(j, u):
                pe.wait_ge(w1_ready, j + 1)
                for i in range(HB):
                    mm = nc.tensor.matmul(bank[:, H_BANK + u, i * P:(i + 1) * P], w1[:, u, i * P:(i + 1) * P],
                                          slotsT[:, bass.ds(j * P, P)], start=True, stop=True)
                mm.then_inc(h_ready, 1)

            def made(j, u):
                pe.wait_ge(h_out, j + 1)
                pe.wait_ge(w2_ready, j + 1)
                pe.wait_ge(y_out, j + (1 - R + FREE))
                for i in range(HB):
                    mm = nc.tensor.matmul(bank[:, Y_BANK + u, 0:D], hT[:, u, i * P:(i + 1) * P], w2[:, u, i * D:(i + 1) * D],
                                          start=(i == 0), stop=(i == HB - 1))
                mm.then_inc(y_ready, 1)

            pe.wait_ge(xT_out, NT)
            hidden(0, 0)
            with pe.Fori(0, TURNS - 1, 1) as i:
                for u in range(R):
                    hidden(i * R + (u + 1), (u + 1) % R)
                    made(i * R + u, u)
            for j in range((TURNS - 1) * R, SLOT_TILES):
                if j + 1 < SLOT_TILES:
                    hidden(j + 1, (j + 1) % R)
                made(j, j % R)

        @block.gpsimd
        def _(pool):
            for h in range(2):
                for par in range(2):
                    other = (1 - h) * HEAD_ROWS
                    pool.memset(k.keys[par][h][other:other + HEAD_ROWS, :], 0.0).then_inc(cleared, 1)
                pool.wait_ge(cleared, 2 * h + 2)
            for par in range(2):
                pool.memset(k.values[par][:, :, :, DK + 1:32], 0.0)
                pool.memset(k.values[par][:, :, :, DK:DK + 1], 1.0)

        @block.vector
        def _(dve):
            dve.sem_inc(y_ready, FREE)
            dve.sem_inc(y_out, FREE)
            dve.wait_ge(k.experts_in, 32)
            with dve.Fori(0, TURNS, 1) as i:
                for u in range(R):
                    j = i * R + u
                    at = dve.value_load(r.weight_at[0:1, bass.ds(j, 1)], min_val=0, max_val=(EXPERTS - 1) * r.hidden)
                    dve.wait_ge(y_ready, j + (1 - R + FREE))
                    dve.sem_inc(copy_allowed, 1)
                    nc.vector.tensor_copy(w1[:, u, :], W1[:, bass.ds(at, r.hidden)]).then_inc(w1_ready, 1)
                    nc.vector.tensor_copy(w2[:, u, :], W2[:, bass.ds(at, HB * D)]).then_inc(w2_ready, 1)

        @block.scalar
        def _(act):
            for n in range(NT):
                act.wait_ge(x_turned, n + 1)
                nc.scalar.activation(slotsT[:, n * CHUNK:n * CHUNK + in_bank(n) * P], bank[:, T_BANK + n % T_BANKS, 0:in_bank(n) * P],
                                     ACT.Copy).then_inc(xT_out, 1)

            def relu(j, u):
                act.wait_ge(h_ready, j + 1)
                nc.scalar.activation(hT[:, u, :], bank[:, H_BANK + u, 0:HB * P], ACT.Relu).then_inc(h_out, 1)

            def keep(j, u):
                act.wait_ge(y_ready, j + (1 + FREE))
                nc.scalar.activation(slots[:, bass.ds(j, 1), :].rearrange("p a d -> p (a d)"), bank[:, Y_BANK + u, 0:D],
                                     ACT.Copy).then_inc(y_out, 1)

            relu(0, 0)
            with act.Fori(0, TURNS - 1, 1) as i:
                for u in range(R):
                    relu(i * R + (u + 1), (u + 1) % R)
                    keep(i * R + u, u)
            for j in range((TURNS - 1) * R, SLOT_TILES):
                if j + 1 < SLOT_TILES:
                    relu(j + 1, (j + 1) % R)
                keep(j, j % R)


def experts(k, tag, W1, W2, gT, hidden, out, b1=None, b2=None, gTf=None):
    nc = k.nc
    bank, xnT = k.bank, k.xnT
    HB = hidden // P
    K = EXPERTS * HB
    R = 4
    with ExitStack() as ctx:
        sem = stage_semaphores(k, ctx, f"{tag}_")
        sb = lambda name, shape, dt=F32: ctx.enter_context(nc.sbuf_tensor(f"{tag}_{name}", shape, dt))
        gs = sb("gate", [P, 2, CHUNK])
        hs = sb("hidden", [P, R, CHUNK])
        hg = sb("gated", [P, R, CHUNK])
        g_ready, g_out, h_ready, h_out, hg_out, hg_used, y_out = (
            sem(n) for n in ("g_ready", "g_out", "h_ready", "h_out", "hg_out", "hg_used", "y_out"))
        block = ctx.enter_context(nc.Block())
        G_BANK, H_BANK, Y_BANK = (1, 2), (3, 4, 5, 7), 6
        LAG = 2
        G_FREE, H_FREE, HG_FREE, USED_FREE, Y_FREE = 2, R, 2 * HB, R, 1

        @block.tensor
        def _(pe):
            k.wait_late(pe)
            with pe.Fori(0, CHUNKS, 1) as i:
                x_in = xnT[:, bass.ds(i * CHUNK, CHUNK)]

                def second(n):
                    if n == 0:
                        pe.wait_ge(y_out, i + Y_FREE)
                        if b2 is not None:
                            nc.tensor.matmul(bank[:, Y_BANK, :], b2[:, :], gTf[:, bass.ds(i * CHUNK, CHUNK)],
                                             start=True, stop=False)
                    pe.wait_ge(hg_out, i * K + (n + 1 + HG_FREE))
                    mm = nc.tensor.matmul(bank[:, Y_BANK, :], W2[:, n, :], hg[:, n % R, :],
                                          start=(n == 0 and b2 is None), stop=(n == K - 1))
                    mm.then_inc(hg_used, 1)

                for n in range(K):
                    e, hb = n // HB, n % HB
                    if hb == 0:
                        pe.wait_ge(g_out, i * EXPERTS + (e - 1 + G_FREE))
                    pe.wait_ge(h_out, i * K + (n - R + 1 + H_FREE))
                    nc.tensor.matmul(bank[:, H_BANK[n % R], :], W1[:, n * P:(n + 1) * P], x_in,
                                     start=True, stop=True).then_inc(h_ready, 1)
                    if hb == 0:
                        nc.tensor.matmul(bank[:, G_BANK[e % 2], :], k.expert_rows[:, e, :], gT[:, bass.ds(i * CHUNK, CHUNK)],
                                         start=True, stop=True).then_inc(g_ready, 1)
                    if n >= LAG:
                        second(n - LAG)
                for n in range(K - LAG, K):
                    second(n)

        @block.scalar
        def _(act):
            k.wait_late(act)
            act.sem_inc(g_out, G_FREE)
            act.sem_inc(h_out, H_FREE)
            act.sem_inc(y_out, Y_FREE)
            with act.Fori(0, CHUNKS, 1) as i:
                for n in range(K):
                    e, hb = n // HB, n % HB
                    if hb == 0:
                        act.wait_ge(g_ready, i * EXPERTS + (e + 1))
                        act.wait_ge(hg_out, i * K + ((e - 1) * HB + HG_FREE))
                        nc.scalar.activation(gs[:, e % 2, :], bank[:, G_BANK[e % 2], :], ACT.Copy).then_inc(g_out, 1)
                    act.wait_ge(h_ready, i * K + (n + 1))
                    act.wait_ge(hg_out, i * K + (n - R + 1 + HG_FREE))
                    if b1 is None:
                        ins = nc.scalar.activation(hs[:, n % R, :], bank[:, H_BANK[n % R], :], ACT.Relu)
                    else:
                        ins = nc.scalar.activation(hs[:, n % R, :], bank[:, H_BANK[n % R], :], ACT.Relu, bias=b1[:, n:n + 1])
                    ins.then_inc(h_out, 1)
                act.wait_ge(hg_used, i * K + (K + USED_FREE))
                nc.scalar.activation(out[:, bass.ds(i * CHUNK, CHUNK)], bank[:, Y_BANK, :], ACT.Silu).then_inc(y_out, 1)

        @block.vector
        def _(dve):
            dve.sem_inc(hg_out, HG_FREE)
            with dve.Fori(0, CHUNKS, 1) as i:
                for n in range(K):
                    e = n // HB
                    dve.wait_ge(g_out, i * EXPERTS + (e + 1 + G_FREE))
                    dve.wait_ge(h_out, i * K + (n + 1 + H_FREE))
                    dve.wait_ge(hg_used, i * K + (n - R + 1 + USED_FREE))
                    nc.vector.tensor_tensor(hg[:, n % R, :], hs[:, n % R, :], gs[:, e % 2, :], ALU.mult).then_inc(hg_out, 1)

        @block.gpsimd
        def _(pool):
            pool.sem_inc(hg_used, USED_FREE)


def add_gated(k, sT, gT):
    nc = k.nc
    bank = k.bank
    with ExitStack() as ctx:
        sem = stage_semaphores(k, ctx, "add_")
        product, turned, added = sem("product"), sem("turned"), sem("added")
        block = ctx.enter_context(nc.Block())

        @block.vector
        def _(dve):
            for c in range(CHUNKS + 1):
                if c < CHUNKS:
                    at = slice(c * CHUNK, (c + 1) * CHUNK)
                    nc.vector.tensor_tensor(sT[:, at], sT[:, at], gT[:, at], ALU.mult).then_inc(product, 1)
                if c:
                    dve.wait_ge(turned, c)
                    x = k.x[:, (c - 1) * TPC:c * TPC, :].rearrange("p t d -> p (t d)")
                    nc.vector.tensor_tensor(x, x, bank[:, (c - 1) % 8, :], ALU.add).then_inc(added, 1)

        @block.tensor
        def _(pe):
            for c in range(CHUNKS):
                pe.wait_ge(product, c + 1)
                for t in range(TPC):
                    at = (c * TPC + t) * P
                    mm = nc.tensor.transpose(bank[:, c % 8, t * P:(t + 1) * P], sT[:, at:at + P], k.ident[:, :])
                mm.then_inc(turned, 1)


SEG = 8
Q_PLACES = dict(first=(0, 8), again=48, second=(16, 8), third=56)
K_PLACES = dict(first=(0, 16), again=56, second=(8, 16), third=48)


def attention_operands(k, b, w, QT, KT, V, attn):
    nc = k.nc
    bank, xnT = k.bank, k.xnT
    NG = SEQ // CHUNK
    UNITS = 2 * NG
    with ExitStack() as ctx:
        sem = stage_semaphores(k, ctx, f"op{b}_", again=b == 0)
        sb = lambda name, shape, dt=F32: ctx.enter_context(nc.sbuf_tensor(f"op{b}_{name}", shape, dt))
        qks = [sb(f"qk{i}", [P, 2, TPC, HEADS, DK]) for i in range(2)]
        rests = [sb(f"rest{i}", [P, 2, TPC, HEADS, DK]) for i in range(2)]
        rot = attn[:, :, :].rearrange("p t d -> p (t d)").rearrange("p (m i t h e) -> p m i t h e", m=4, i=2, t=TPC, h=HEADS)
        st = sb("st", [P, 3, 2, TPC, HEADS])
        total, root, rstd = (st[:, i] for i in range(3))
        split = sb("split", [P, 2, TPC, HEADS, HEAD_ROWS], BF16)
        (cleared, projected, squared, stat, rooted, scaled, weighted, turned_q, cast1, left1, cast2, split_ready,
         v_out, turned, taken_a, taken_d) = (
            sem(n) for n in ("cleared", "projected", "squared", "stat", "rooted", "scaled", "weighted", "roped",
                             "cast1", "left1", "cast2", "split_ready", "v_out", "turned", "taken_a", "taken_d"))
        block = ctx.enter_context(nc.Block())
        proj = bank[:, 0:TPC, :]
        qk_psum = [proj[:, :, i * D:(i + 1) * D].rearrange("p t (h e) -> p t h e", e=DK) for i in range(2)]
        flat = lambda t, i: t[:, i].rearrange("p t h e -> p (t h) e")

        @block.tensor
        def _(pe):
            k.wait_late(pe)

            def project(g):
                if g:
                    pe.wait_ge(scaled, 2 * g)
                    pe.wait_ge(v_out, g)
                for t in range(TPC):
                    at = SEQ * b + g * CHUNK + t * P
                    mm = nc.tensor.matmul(bank[:, t, 0:3 * D], xnT[:, at:at + P], w.wqkv[:, :], start=True, stop=True)
                mm.then_inc(projected, 1)

            project(0)
            pe.wait_ge(cleared, 3)
            for g in range(NG):
                if g + 1 < NG:
                    project(g + 1)
                for i in range(2):
                    pe.wait_ge(split_ready, 2 * g + i + 1)
                    for n in range(PAIRS // 2):
                        m = 8 * g + 4 * i + n
                        if m >= 4:
                            pe.wait_ge(taken_a if m % 2 == 0 else taken_d, (m - 4) // 2 + 1)
                        out = bank[:, 4 + n, :].bitcast(BF16)
                        for j in range(2):
                            for t in range(TPC):
                                mm = nc.tensor.transpose(
                                    out[:, (j * TPC + t) * P:(j * TPC + t + 1) * P],
                                    split[:, i, t, 2 * (2 * n + j):2 * (2 * n + j) + 2, :].rearrange("p h r -> p (h r)"),
                                    k.identb[:, :])
                        mm.then_inc(turned, 1)

        def taken(eng, copy, parity, done):
            def run(u, turn):
                if u >= 0:
                    g, i = divmod(u, 2)
                    n = 2 * turn + parity
                    eng.wait_ge(turned, 4 * u + n + 1)
                    copy((QT, KT)[i][:, 2 * n:2 * n + 2, g * CHUNK:(g + 1) * CHUNK],
                         bank[:, 4 + n, :].bitcast(BF16).rearrange("p (j t) -> p j t", j=2)).then_inc(done, 1)
            return run

        @block.scalar
        def _(act):
            take = taken(act, lambda o, i: nc.scalar.activation(o, i, ACT.Copy), 0, taken_a)

            def square(g):
                act.wait_ge(projected, g + 1)
                if g >= 2:
                    act.wait_ge(split_ready, 2 * (g - 1))
                for i in range(2):
                    nc.scalar.activation(rests[g % 2][:, i], qk_psum[i], ACT.Square).then_inc(squared, 1)
                nc.scalar.activation(V[:, g * TPC:(g + 1) * TPC, :], proj[:, :, 2 * D:3 * D], ACT.Copy).then_inc(v_out, 1)

            def take_root(g):
                act.wait_ge(stat, 2 * g + 2)
                nc.scalar.activation(root[:, :, :, :], total[:, :, :, :], ACT.Sqrt).then_inc(rooted, 1)

            square(0)
            take_root(0)
            act.wait_ge(cleared, 3)
            for u in range(UNITS):
                g, i = divmod(u, 2)
                places = (Q_PLACES, K_PLACES)[i]
                s = flat(split, i)
                if i == 1 and g + 1 < NG:
                    take_root(g + 1)
                act.wait_ge(turned_q, u + 1)
                if u >= 2:
                    act.wait_ge(turned, 4 * (u - 1))
                at, step = places["first"]
                src = flat(qks[g % 2], i)
                nc.scalar.activation(s[:, :, at:at + 8], src, ACT.Copy).then_inc(cast1, 1)
                nc.scalar.activation(s[:, :, at + step:at + step + 8], src, ACT.Copy).then_inc(cast1, 1)
                nc.scalar.activation(s[:, :, places["again"]:places["again"] + 8], src, ACT.Copy).then_inc(cast1, 1)
                take(u - 1, 0)
                act.wait_ge(left1, u + 1)
                at, step = places["second"]
                src = flat(rests[g % 2], i)
                nc.scalar.activation(s[:, :, at:at + 8], src, ACT.Copy).then_inc(cast2, 1)
                nc.scalar.activation(s[:, :, at + step:at + step + 8], src, ACT.Copy).then_inc(cast2, 1)
                take(u - 1, 1)
                if i == 0 and g + 1 < NG:
                    square(g + 1)
            for turn in range(2):
                take(UNITS - 1, turn)

        @block.gpsimd
        def _(pool):
            pool.memset(split[:, :, :, :, :], 0.0).then_inc(cleared, 1)
            pool.wait_ge(cleared, 1)
            pool.memset(split[:, 1, :, :, SHIFT:SHIFT + PARTS], 1.0).then_inc(cleared, 1)
            pool.memset(attn[:, :, :], 0.0).then_inc(cleared, 1)
            k.wait_late(pool)

            def weight(g):
                for i in range(2):
                    pool.wait_ge(scaled, 2 * g + i + 1)
                    qk = qks[g % 2]
                    nc.gpsimd.tensor_tensor(flat(qk, i), flat(qk, i), bc(w.norm_w[:, i, :].unsqueeze(1), [P, TPC * HEADS, DK]),
                                            ALU.mult).then_inc(weighted, 1)

            for g in range(NG):
                weight(g)


        @block.vector
        def _(dve):
            k.wait_late(dve)
            take = taken(dve, nc.vector.tensor_copy, 1, taken_d)
            tt = nc.vector.tensor_tensor
            steps = sem("rope_step")
            n = 0

            def statistics(g):
                nonlocal n
                for i in range(2):
                    dve.wait_ge(squared, 2 * g + i + 1)
                    nc.vector.tensor_reduce(total[:, i], rests[g % 2][:, i], X_AXIS, ALU.add).then_inc(steps, 1)
                    n += 1
                dve.wait_ge(steps, n)
                for i in range(2):
                    nc.vector.tensor_scalar(total[:, i], total[:, i], 1.0 / DK, EPS, ALU.mult, ALU.add).then_inc(stat, 1)

            def scale(g):
                nonlocal n
                dve.wait_ge(rooted, g + 1)
                nc.vector.reciprocal(rstd[:, :, :, :], root[:, :, :, :]).then_inc(steps, 1)
                n += 1
                dve.wait_ge(steps, n)
                if g >= 2:
                    dve.wait_ge(cast1, 6 * (g - 1))
                for i in range(2):
                    tt(qks[g % 2][:, i], qk_psum[i], bc(rstd[:, i].unsqueeze(3), [P, TPC, HEADS, DK]), ALU.mult).then_inc(scaled, 1)

            statistics(0)
            scale(0)
            dve.wait_ge(cleared, 3)
            for u in range(UNITS):
                g, i = divmod(u, 2)
                qk, rest = qks[g % 2], rests[g % 2]
                places = (Q_PLACES, K_PLACES)[i]
                s = flat(split, i)
                dve.wait_ge(weighted, u + 1)
                if g == NG - 1:
                    x0 = qk[:, i, :, :, 0:DK:2]
                    x1 = qk[:, i, :, :, 1:DK:2]
                    wide = [P, TPC, HEADS, DK // 2]
                    cos, sin = (bc(r[:, :, :].unsqueeze(2), wide) for r in (w.cos, w.sin))
                    for m, (a, f) in enumerate(((x0, cos), (x1, sin), (x0, sin), (x1, cos))):
                        tt(rot[:, m, i], a, f, ALU.mult).then_inc(steps, 1)
                    n += 4
                    dve.wait_ge(steps, n)
                    tt(x0, rot[:, 0, i], rot[:, 1, i], ALU.subtract).then_inc(steps, 1)
                    tt(x1, rot[:, 2, i], rot[:, 3, i], ALU.add).then_inc(steps, 1)
                    n += 2
                    dve.wait_ge(steps, n)
                nc.vector.tensor_scalar(qk[:, i], qk[:, i], DK ** -0.5 if i == 0 else 1.0, None, ALU.mult).then_inc(turned_q, 1)
                if i == 1 and g + 1 < NG:
                    scale(g + 1)
                take(u - 1, 0)
                dve.wait_ge(cast1, 3 * u + 3)
                at = places["first"][0]
                tt(flat(rest, i), flat(qk, i), s[:, :, at:at + 8], ALU.subtract).then_inc(left1, 1)
                take(u - 1, 1)
                dve.wait_ge(cast2, 2 * u + 2)
                at = places["second"][0]
                tt(s[:, :, places["third"]:places["third"] + 8], flat(rest, i), s[:, :, at:at + 8],
                   ALU.subtract).then_inc(split_ready, 1)
                if i == 0 and g + 1 < NG:
                    statistics(g + 1)
            for turn in range(2):
                take(UNITS - 1, turn)


def softmax_attention(k, b, QT, KT, V, attn, gather=None):
    nc = k.nc
    bank = k.bank
    NK = SEQ // P
    QC = SEQ // CHUNK
    UNROLL = 2
    S = 2 * NK
    R = 3
    PR = 8
    S_BANK, M_BANK, O_BANK, T_BANK = 0, 3, 6, 7
    AHEAD = 24
    SHIFTS_AFTER = 6
    with ExitStack() as ctx:
        sem = stage_semaphores(k, ctx, f"at{b}_", again=b == 0)
        sb = lambda name, shape, dt=F32: ctx.enter_context(nc.sbuf_tensor(f"at{b}_{name}", shape, dt))
        queries, keys, values = k.queries, k.keys, k.values
        probs = sb("probs", [P, PR, CHUNK])
        tops = sb("tops", [P, 2, 2 * TPC, QC])
        neg = sb("neg", [P, 2 * TPC])
        left = sb("left", [P, 2, 2 * TPC])
        shift = sb("shift", [P, TPC, P], BF16)
        sumsT = sb("sumsT", [P, CHUNK])
        inv = sb("inv", [P, 2 * TPC])
        (cleared, copy_allowed, q_loaded, k_loaded, v_loaded, m_ready, m_out, neg_ready, shift_step, shift_ready, shiftT_ready,
         shift_in, s_ready, p_ready, p_used, sums_out, turned, inv_ready, attn_out) = (
            sem(n) for n in ("cleared", "copy_allowed", "q_loaded", "k_loaded", "v_loaded", "m_ready", "m_out", "neg_ready",
                             "shift_step", "shift_ready", "shiftT_ready", "shift_in", "s_ready", "p_ready", "p_used",
                             "sums_out", "turned", "inv_ready", "attn_out"))
        block = ctx.enter_context(nc.Block())
        GATHERED = TILES // (UNROLL * QC)
        M_FREE, P_FREE, U_FREE, O_FREE, T_FREE = R, R, PR // 4, 1, 1
        G = 4

        ahead = Core()
        ahead.turn = None

        def two_on(n):
            return Step(ahead.turn, n.per_turn, n.number + 2 - (0 if n.turn is None else n.per_turn))

        def turns(eng, body):
            with eng.Fori(0, PAIRS // UNROLL - 1, 1) as i:
                ahead_i = eng.snap(i + 1)
                for u in range(UNROLL):
                    ahead.turn = ahead_i
                    body(Step(i, UNROLL, u), Step(i, UNROLL * QC, u * QC), u, False)
            ahead.turn = None
            for u in range(UNROLL):
                body(Step(None, 0, PAIRS - UNROLL + u), Step(None, 0, (PAIRS - UNROLL + u) * QC), u, u == UNROLL - 1)

        @block.gpsimd
        def _(pool):
            pool.memset(shift[:, :, :], 0.0).then_inc(cleared, 1)
            pool.sem_inc(m_out, M_FREE)
            pool.sem_inc(p_ready, P_FREE)
            pool.sem_inc(p_used, U_FREE)
            pool.sem_inc(sums_out, O_FREE)
            pool.sem_inc(attn_out, T_FREE)

            def before_copy():
                pool.sem_inc(copy_allowed, 1)

            def load(pair, par):
                before_copy()
                chosen = lambda t, rows: t[rows, bass.ds(pair.at(1, 0), 1), :].rearrange("p a t -> p (a t)")
                nc.gpsimd.tensor_copy(queries[par][:, :], chosen(QT, slice(0, P))).then_inc(q_loaded, 1)
                pool.wait_ge(q_loaded, pair.at(1, 1))
                for h in range(2):
                    rows = slice(h * HEAD_ROWS, (h + 1) * HEAD_ROWS)
                    before_copy()
                    nc.gpsimd.tensor_copy(keys[par][h][rows, :], chosen(KT, rows)).then_inc(k_loaded, 1)
                    pool.wait_ge(k_loaded, pair.at(2, h + 1))
                before_copy()
                for h in range(2):
                    src = V[:, :, bass.ds(pair.at(2 * DK, h * DK), DK)]
                    nc.gpsimd.tensor_copy(values[par][:, :, h, 0:DK], src).then_inc(v_loaded, 1)

            def parts(m):
                pool.wait_ge(neg_ready, m.at(1, 1))
                if m.turn is not None or m.number > 0:
                    pool.wait_ge(shiftT_ready, m.at(1, 0))
                place = lambda i: shift[:, :, :].rearrange("p t (h r) -> p h t r", h=2)[:, :, :, SHIFT + i]
                src = neg[:, :].rearrange("p (h t) -> p h t", h=2)
                rest = [left[:, i, :].rearrange("p (h t) -> p h t", h=2) for i in range(2)]
                before_copy()
                nc.gpsimd.tensor_copy(place(0), src).then_inc(shift_step, 1)
                pool.wait_ge(shift_step, m.at(4, 1))
                nc.gpsimd.tensor_tensor(rest[0], src, place(0), ALU.subtract).then_inc(shift_step, 1)
                pool.wait_ge(shift_step, m.at(4, 2))
                before_copy()
                nc.gpsimd.tensor_copy(place(1), rest[0]).then_inc(shift_step, 1)
                pool.wait_ge(shift_step, m.at(4, 3))
                nc.gpsimd.tensor_tensor(rest[1], rest[0], place(1), ALU.subtract).then_inc(shift_step, 1)
                pool.wait_ge(shift_step, m.at(4, 4))
                before_copy()
                nc.gpsimd.tensor_copy(place(2), rest[1]).then_inc(shift_ready, 1)

            pool.wait_ge(cleared, 1)
            for h in range(2):
                nc.gpsimd.tensor_copy(values[0][:, :, h, 0:DK], V[:, :, h * DK:(h + 1) * DK]).then_inc(v_loaded, 1)
            parts(Step(None, 0, 0))

            def pair_steps(pair, chunk, par, final):
                for c in range(QC):
                    if not (final and c == QC - 1):
                        parts(chunk + (c + 1))
                    if c == 0 and not final:
                        pool.wait_ge(p_used, pair.at(QC * S // G, U_FREE))
                        load(pair + 1, 1 - par)
                    if gather is not None and pair.turn is None:
                        first = ((pair.number - (PAIRS - UNROLL)) * QC + c) * GATHERED
                        for t in range(first, first + GATHERED):
                            gather(pool, t)

            turns(pool, pair_steps)

        def earlier(s):
            return next(d for d in range(1, 2 * R + 1) if (s - d) % S % R == s % R and (s >= d or (s - d + S) % R == s % R))

        @block.tensor
        def _(pe):
            pe.wait_ge(cleared, 1)

            def for_maxima(m, c, par, a):
                h, qt, kb = a // (TPC * QC), a // QC % TPC, a % QC
                pe.wait_ge(m_out, m.at(S, a - earlier(a) + 1 + M_FREE))
                at = (c * TPC + qt) * P
                nc.tensor.matmul(bank[:, M_BANK + a % R, :], queries[par][:, at:at + P],
                                 keys[par][h][:, kb * CHUNK:(kb + 1) * CHUNK], start=True, stop=True).then_inc(m_ready, 1)

            def shifts(m):
                pe.wait_ge(shift_ready, m.at(1, 1))
                if m.turn is not None or m.number > 1:
                    pe.wait_ge(attn_out, m.at(1, T_FREE - 1))
                out = bank[:, T_BANK, :].bitcast(BF16)
                for t in range(TPC):
                    mm = nc.tensor.transpose(out[:, t * P:(t + 1) * P], shift[:, t, :], k.identb[:, :])
                mm.then_inc(shiftT_ready, 1)

            def score(n, c, par, s):
                pe.wait_ge(p_ready, n.at(S, s - earlier(s) + 1 + P_FREE))
                nc.tensor.matmul(bank[:, S_BANK + s % R, :], keys[par][s % 2][:, (s // 2) * P:(s // 2 + 1) * P],
                                 queries[par][:, c * CHUNK:(c + 1) * CHUNK], start=True, stop=True).then_inc(s_ready, 1)

            def weigh(n, par, g):
                if g == 0:
                    pe.wait_ge(sums_out, n.at(1, O_FREE))
                pe.wait_ge(p_ready, n.at(S, 4 * g + 4 + P_FREE))
                for j in range(G):
                    s = G * g + j
                    mm = nc.tensor.matmul(bank[32 * j:32 * j + 32, O_BANK, :], values[par][:, s // 2, s % 2, :],
                                          probs[:, s % PR, :], start=(g == 0), stop=(g == S // G - 1),
                                          tile_position=(0, 32 * j))
                mm.then_inc(p_used, 1)

            zero = Step(None, 0, 0)
            pe.wait_ge(q_loaded, 1)
            pe.wait_ge(k_loaded, 2)
            for a in range(S):
                for_maxima(zero, 0, 0, a)
            for a in range(AHEAD):
                for_maxima(zero + 1, 1, 0, a)
                if a == AHEAD // 2:
                    shifts(zero)
            pe.wait_ge(shift_in, 2)
            for s in range(2 * G):
                score(zero, 0, 0, s)
            pe.wait_ge(v_loaded, 2)
            weigh(zero, 0, 0)

            def pair_steps(pair, chunk, par, final):
                for c in range(QC):
                    n = chunk + c
                    last, last_two = final and c == QC - 1, final and c >= QC - 2
                    next_par = par if c < QC - 1 else 1 - par
                    pending = [] if last else [(n + 1, (c + 1) % QC, next_par, a) for a in range(AHEAD, S)]
                    if not last_two:
                        m_par = par if c < QC - 2 else 1 - par
                        pending += [(two_on(n), (c + 2) % QC, m_par, a) for a in range(AHEAD)]

                    def maximum():
                        if pending:
                            m, m_c, m_p, a = pending.pop(0)
                            if a == 0 and m_c == 0:
                                pe.wait_ge(q_loaded, pair.at(1, 2))
                                pe.wait_ge(k_loaded, pair.at(2, 4))
                            for_maxima(m, m_c, m_p, a)

                    for g in range(2, S // G):
                        for j in range(G):
                            score(n, c, par, G * g + j)
                            maximum()
                        if g == SHIFTS_AFTER and not last:
                            shifts(n + 1)
                        weigh(n, par, g - 1)
                    if not last:
                        pe.wait_ge(shift_in, n.at(2, 4))
                        for s in range(G):
                            score(n + 1, (c + 1) % QC, next_par, s)
                            maximum()
                    weigh(n, par, S // G - 1)
                    if not last:
                        for s in range(G, 2 * G):
                            score(n + 1, (c + 1) % QC, next_par, s)
                            maximum()
                    pe.wait_ge(attn_out, n.at(1, T_FREE))
                    pe.wait_ge(sums_out, n.at(1, 1 + O_FREE))
                    for t in range(TPC):
                        mm = nc.tensor.matmul(bank[:, T_BANK, 256 + 18 * t:256 + 18 * (t + 1)], sumsT[:, t * P:(t + 1) * P],
                                              k.sum_parity[:, :], start=True, stop=True)
                    mm.then_inc(turned, 1)
                    if not last:
                        if c == QC - 1:
                            pe.wait_ge(v_loaded, pair.at(2, 4))
                        weigh(n + 1, next_par, 0)

            turns(pe, pair_steps)

        @block.scalar
        def _(act):
            def take_shifts(m, par, c):
                act.wait_ge(shiftT_ready, m.at(1, 1))
                for h in range(2):
                    rows = slice(h * HEAD_ROWS + SHIFT, h * HEAD_ROWS + SHIFT + PARTS)
                    nc.scalar.activation(queries[par][rows, c * CHUNK:(c + 1) * CHUNK],
                                         bank[rows, T_BANK, 0:CHUNK // 2].bitcast(BF16), ACT.Copy).then_inc(shift_in, 1)

            def exponential(n, s):
                act.wait_ge(s_ready, n.at(S, s + 1))
                if s % G == 0:
                    act.wait_ge(p_used, n.at(S // G, s // G - 1 + U_FREE))
                nc.scalar.activation(probs[:, s % PR, :], bank[:, S_BANK + s % R, :], ACT.Exp).then_inc(p_ready, 1)

            take_shifts(Step(None, 0, 0), 0, 0)
            for s in range(G):
                exponential(Step(None, 0, 0), s)

            def pair_steps(pair, chunk, par, final):
                for c in range(QC):
                    n = chunk + c
                    for s in range(G, S):
                        exponential(n, s)
                        if s == G * (SHIFTS_AFTER + 1) - 1 and not (final and c == QC - 1):
                            take_shifts(n + 1, par if c < QC - 1 else 1 - par, (c + 1) % QC)
                    if not (final and c == QC - 1):
                        for s in range(G):
                            exponential(n + 1, s)
                    act.wait_ge(p_used, n.at(S // G, S // G + U_FREE))
                    nc.scalar.activation(sumsT[:, :], bank[:, O_BANK, :], ACT.Copy).then_inc(sums_out, 1)

            turns(act, pair_steps)

        @block.vector
        def _(dve):
            TAKEN = AHEAD

            def maxima(m, of):
                for a in of:
                    dve.wait_ge(m_ready, m.at(S, a + 1))
                    nc.vector.tensor_reduce(tops[:, m.number % 2, a // QC, a % QC:a % QC + 1], bank[:, M_BANK + a % R, :], X_AXIS,
                                            ALU.max).then_inc(m_out, 1)

            def negate(m):
                if m.turn is not None or m.number > 0:
                    dve.wait_ge(shift_ready, m.at(1, 0))
                dve.wait_ge(m_out, m.at(S, S + M_FREE))
                nc.vector.tensor_reduce(neg[:, :], tops[:, m.number % 2], X_AXIS, ALU.max, negate=True).then_inc(neg_ready, 1)

            nc.vector.tensor_copy(queries[0][:, :], QT[:, 0, :]).then_inc(q_loaded, 1)
            for h in range(2):
                rows = slice(h * HEAD_ROWS, (h + 1) * HEAD_ROWS)
                nc.vector.tensor_copy(keys[0][h][rows, :], KT[rows, 0, :]).then_inc(k_loaded, 1)
            maxima(Step(None, 0, 0), range(S))
            negate(Step(None, 0, 0))
            maxima(Step(None, 0, 1), range(TAKEN + 1))

            def pair_steps(pair, chunk, par, final):
                for c in range(QC):
                    n = chunk + c
                    if not (final and c == QC - 1):
                        maxima(n + 1, range(TAKEN + 1, S))
                    if not (final and c == QC - 1):
                        negate(n + 1)
                    if not (final and c >= QC - 2):
                        maxima(two_on(n), range(TAKEN))
                    dve.wait_ge(turned, n.at(1, 1))
                    sums = bank[:, T_BANK, 256:256 + 18 * TPC].rearrange("p (t h e) -> p t h e", h=2, e=DK + 1)
                    nc.vector.reciprocal(inv[:, :].rearrange("p (t h) -> p t h", h=2), sums[:, :, :, DK]).then_inc(inv_ready, 1)
                    if not (final and c >= QC - 2):
                        maxima(two_on(n), range(TAKEN, TAKEN + 1))
                    dve.wait_ge(inv_ready, n.at(1, 1))
                    to = attn[:, c * TPC:(c + 1) * TPC, bass.ds(pair.at(2 * DK, 0), 2 * DK)]
                    nc.vector.tensor_tensor(to.rearrange("p t (h e) -> p t h e", h=2), sums[:, :, :, 0:DK],
                                            bc(inv[:, :].rearrange("p (t h) -> p t h", h=2).unsqueeze(3), [P, TPC, 2, DK]),
                                            ALU.mult).then_inc(attn_out, 1)

            turns(dve, pair_steps)


def finish(k, b, w, attn, g_rows, r, out_dram):
    nc = k.nc
    bank = k.bank
    NG = SEQ // CHUNK
    with ExitStack() as ctx:
        sem = stage_semaphores(k, ctx, f"fin{b}_", again=b == 0)
        sb = lambda name, shape: ctx.enter_context(nc.sbuf_tensor(f"fin{b}_{name}", shape, F32))
        attnT = sb("attnT", [P, NG, CHUNK])
        product = sb("product", [P, NG, CHUNK])
        g_ready, turned, taken, projected, gated, added = (
            sem(n) for n in ("g_ready", "turned", "taken", "projected", "gated", "added"))
        block = ctx.enter_context(nc.Block())
        out_tiles = out_dram.rearrange("b (t p) d -> p (b t) d", p=P)

        @block.tensor
        def _(pe):
            for c in range(NG + 1):
                if c < NG:
                    for t in range(TPC):
                        mm = nc.tensor.transpose(bank[:, c, t * P:(t + 1) * P], attn[:, c * TPC + t, :], k.ident[:, :])
                    mm.then_inc(turned, 1)
                if c:
                    pe.wait_ge(taken, c)
                    for t in range(TPC):
                        mm = nc.tensor.matmul(bank[:, NG + c - 1, t * P:(t + 1) * P], attnT[:, c - 1, t * P:(t + 1) * P], w.woT[:, :],
                                              start=True, stop=True)
                    mm.then_inc(projected, 1)

        @block.scalar
        def _(act):
            for c in range(NG):
                if c % 2 == 0:
                    act.wait_ge(r.gathered[(b * NG + c) * TPC // GT], 16 * GT)
                for t in range((b * NG + c) * TPC, (b * NG + c + 1) * TPC):
                    ins = nc.scalar.activation(g_rows[:, t, :], g_rows[:, t, :], ACT.Silu, scale=r.gate[:, t:t + 1])
                ins.then_inc(g_ready, 1)
                act.wait_ge(turned, c + 1)
                nc.scalar.activation(attnT[:, c, :], bank[:, c, :], ACT.Copy).then_inc(taken, 1)

        @block.vector
        def _(dve):
            def flat(a, c):
                t0 = (b * NG + c) * TPC
                return a[:, t0:t0 + TPC, :].rearrange("p t d -> p (t d)")

            for c in range(NG):
                dve.wait_ge(projected, c + 1)
                dve.wait_ge(g_ready, c + 1)
                nc.vector.tensor_tensor(product[:, c, :], bank[:, NG + c, :], flat(g_rows, c), ALU.mult).then_inc(gated, 1)
                dve.wait_ge(gated, c + 1)
                nc.vector.tensor_tensor(flat(k.x, c), flat(k.x, c), product[:, c, :], ALU.add).then_inc(added, 1)

        @block.sync
        def _(sp):
            for c in range(NG):
                sp.wait_ge(added, c + 1)
                t0 = (b * NG + c) * TPC
                sp.dma_start(out_tiles[:, t0:t0 + TPC, :], k.x[:, t0:t0 + TPC, :]).then_inc(k.stored, 16)
            if b == BATCH - 1:
                sp.wait_ge(k.stored, 16 * NG * BATCH)


def build(nc, a, out):
    with ExitStack() as whole:
        def sb(ctx, name, shape, dt=F32):
            return ctx.enter_context(nc.sbuf_tensor(name, shape, dt))

        k, w = Core(), Core()
        k.nc = nc
        k.whole = whole
        k.bank = whole.enter_context(nc.psum_tensor("bank", [P, 8, CHUNK], F32))
        k.x = sb(whole, "x", [P, TILES, D])
        k.xnT = sb(whole, "xnT", [P, TOK])
        k.ident = sb(whole, "ident", [P, P])
        k.identb = sb(whole, "identb", [P, P], BF16)
        k.ones = sb(whole, "ones", [P, P])
        k.expert_rows = sb(whole, "expert_rows", [PARTS * EXPERTS, EXPERTS, P], BF16)
        k.sum_parity = sb(whole, "sum_parity", [P, 18])
        k.pair_mask = sb(whole, "pair_mask", [P, 2 * DK])
        k.weight_rank = sb(whole, "weight_rank", [P, EXPERTS])
        w.wqkv = sb(whole, "wqkv", [P, 3 * D])
        w.woT = sb(whole, "woT", [P, D])
        w.norm_w = sb(whole, "norm_w", [P, 2, DK])
        w.cos = sb(whole, "cos", [P, TPC, DK // 2])
        w.sin = sb(whole, "sin", [P, TPC, DK // 2])
        w.Wg1 = sb(whole, "Wg1", [P, EXPERTS])
        w.bg1 = sb(whole, "bg1", [P, EXPERTS])
        early = whole.enter_context(nc.semaphore("early_weights_in"))
        late = whole.enter_context(nc.semaphore("late_weights_in"))
        g_rows = sb(whole, "g_rows", [P, TILES, D])
        g0T = g_rows[:, :, :].rearrange("p t d -> p (t d)")
        k.before = sb(whole, "before", [P, P])
        k.zeros = sb(whole, "zeros", [P, SLOTS * D // P // 8])
        k.number = sb(whole, "number", [P, SLOT_TILES])
        k.tile_start = sb(whole, "tile_start", [P, TILES])
        k.zeros_ready = whole.enter_context(nc.semaphore("zeros_ready"))
        k.gate_in = whole.enter_context(nc.semaphore("block0_gate_in"))
        k.made_stored = whole.enter_context(nc.semaphore("made_stored"))
        k.stored = whole.enter_context(nc.semaphore("out_stored"))
        k.zeros_stored = whole.enter_context(nc.semaphore("zeros_stored"))
        sorted_dram = nc.dram_tensor("sorted_tokens", (SLOTS, D), F32).ap()
        made_dram = nc.dram_tensor("made_of_sorted", (SLOTS, D), F32).ap()
        r = Core()
        r.gathered = [whole.enter_context(nc.semaphore(f"gathered{g}")) for g in range(GROUPS)]

        def gather(pool, t):
            pool.indirect_dma_start(g_rows[:, t, :], None, made_dram,
                                    bass.IndirectOffsetOnAxis(ap=r.slot[:, t:t + 1], axis=0)).then_inc(r.gathered[t // GT], 16)

        r.hidden = a["L1_ffn_W1"].shape[2]
        r.gate = sb(whole, "gate1", [P, TILES])
        r.slot = sb(whole, "slot", [P, TILES], mybir.dt.uint32)
        r.weight_at = sb(whole, "weight_at", [P, SLOT_TILES], mybir.dt.int32)

        hidden0, hidden1 = a["L0_ffn_W1"].shape[2], a["L1_ffn_W1"].shape[2]
        n0, n1 = EXPERTS * hidden0 // P, EXPERTS * hidden1 // P
        first = ExitStack()
        w.Wq, w.Wk, w.Wv = (sb(first, n, [P, D]) for n in ("Wq", "Wk", "Wv"))
        w.Wo = sb(first, "Wo", [P, 2, D])
        w.rw = sb(first, "rw", [P, HEADS * FEAT])
        w.bq, w.bk, w.bo = (sb(first, n, [P, 1]) for n in ("bq", "bk", "bo"))
        w.bv = sb(first, "bv", [P, D])
        Wg0 = sb(first, "Wg0", [P, EXPERTS])
        W10 = sb(first, "W10", [P, EXPERTS * hidden0])
        W20 = sb(first, "W20", [P, n0, D])
        b10 = sb(first, "b10", [P, n0])
        b20 = sb(first, "b20", [PARTS * EXPERTS, D])
        sT = sb(first, "sT", [P, TOK])

        column = lambda v: v.rearrange("(p o) -> p o", o=1)
        spread = lambda v: v.rearrange("(o n) -> o n", o=1).partition_broadcast(P)
        early_loads = [(w.Wq[:, :], a["L0_attn_Wq"]), (w.Wk[:, :], a["L0_attn_Wk"]), (w.Wv[:, :], a["L0_attn_Wv"]),
                       (w.bq[:, :], column(a["L0_attn_bq"])), (w.bk[:, :], column(a["L0_attn_bk"])),
                       (w.bo[:, :], column(a["L0_attn_bo"])), (w.bv[:, :], spread(a["L0_attn_bv"]))]
        early_loads += [(w.rw[DK * h:DK * (h + 1), FEAT * h:FEAT * (h + 1)], a["L0_attn_rw"][h]) for h in range(HEADS)]
        early_loads += [(w.Wo[32 * (j % 4):32 * (j % 4) + 2 * DK, j // 4, :], a["L0_attn_Wo"][2 * DK * j:2 * DK * (j + 1), :])
                        for j in range(PAIRS)]
        late_loads = [(W10[:, :].rearrange("p (e h) -> p e h", e=EXPERTS), a["L0_ffn_W1"].rearrange("e d h -> d e h")),
                      (W20[:, :, :], a["L0_ffn_W2"].rearrange("e (b p) d -> p (e b) d", p=P)),
                      (b10[:, :], a["L0_ffn_b1T"])]
        late_loads += [(b20[EXPERTS * i:EXPERTS * (i + 1), :], a["L0_ffn_b2"]) for i in range(PARTS)]
        late_loads += [(w.Wg1[:, :], a["L1_ffn_Wg"]), (w.bg1[:, :], spread(a["L1_ffn_bg"])),
                       (w.wqkv[:, 0:D], a["L1_attn_wqT"]), (w.wqkv[:, D:2 * D], a["L1_attn_wkT"]),
                       (w.wqkv[:, 2 * D:3 * D], a["L1_attn_wvT"]), (w.woT[:, :], a["L1_attn_woT"]),
                       (w.norm_w[:, 0, :], spread(a["L1_attn_q_norm_w"])), (w.norm_w[:, 1, :], spread(a["L1_attn_k_norm_w"]))]
        lead = TPC * P - ROPE
        for table, name in ((w.cos, "L1_attn_rope_cos"), (w.sin, "L1_attn_rope_sin")):
            late_loads += [(table[lead:P, 0, :], a[name][0:P - lead, :]),
                           (table[:, 1:TPC, :], a[name][P - lead:ROPE, :].rearrange("(t p) f -> p t f", p=P))]

        def load_gate(sp):
            sp.dma_start(Wg0[:, :], a["L0_ffn_Wg"]).then_inc(k.gate_in, 16)

        k.load_gate = load_gate

        def load_weights(sp):
            sp.wait_ge(k.rw_cleared, len(k.clear))
            for to, of in early_loads:
                sp.dma_start(to, of).then_inc(early, 16)
            sp.wait_ge(k.zeros_ready, 1)
            zero_rows = sorted_dram.rearrange("a d -> (a d)").rearrange("(i p f) -> i p f", i=8, p=P)
            for i in range(8):
                sp.dma_start(zero_rows[i], k.zeros[:, :]).then_inc(k.zeros_stored, 16)
            for to, of in late_loads:
                sp.dma_start(to, of).then_inc(late, 16)

        k.load_weights = load_weights
        k.wait_weights = lambda eng: eng.wait_ge(early, 16 * len(early_loads))
        k.wait_late = lambda eng: eng.wait_ge(late, 16 * len(late_loads))
        k.clear = [(w.rw[:, :], 0.0), (w.Wo[:, :, :], 0.0), (w.cos[:, :, :], 1.0), (w.sin[:, :, :], 0.0)]

        k.cleared = whole.enter_context(nc.semaphore("constants_cleared"))
        k.rw_cleared = whole.enter_context(nc.semaphore("weights_cleared"))
        k.x_in = [whole.enter_context(nc.semaphore(f"x_in{g}")) for g in range(GROUPS)]
        normalise(k, "ln0", Wg0, lambda pe: pe.wait_ge(k.gate_in, 16), load=k.load_weights, x_dram=a["L0_attn_x"])
        with ExitStack() as ctx:
            gT = sb(ctx, "g0_parts", [PARTS * EXPERTS, TOK], BF16)
            gTf = sb(ctx, "g0_parts32", [PARTS * EXPERTS, TOK])
            gates(k, "gate0", gT, gTf)
            linear_attention(k, w, sT)
            experts(k, "ffn0", W10, W20, gT, hidden0, g0T, b10, b20, gTf)
        add_gated(k, sT, g0T)
        first.close()
        k.queries = [sb(whole, f"queries{i}", [P, SEQ], BF16) for i in range(2)]
        k.keys = [[sb(whole, f"keys{i}{h}", [P, SEQ], BF16) for h in range(2)] for i in range(2)]
        k.values = [sb(whole, f"values{i}", [P, SEQ // P, 2, 32]) for i in range(2)]
        second = ExitStack()
        W11 = sb(second, "W11", [P, EXPERTS * hidden1])
        W21 = sb(second, "W21", [P, n1, D])
        k.experts_in = whole.enter_context(nc.semaphore("block1_experts_in"))

        def load_experts(sp):
            sp.dma_start(W11[:, :].rearrange("p (e h) -> p e h", e=EXPERTS), a["L1_ffn_W1"].rearrange("e d h -> d e h")).then_inc(k.experts_in, 16)
            sp.dma_start(W21[:, :, :], a["L1_ffn_W2"].rearrange("e (b p) d -> p (e b) d", p=P)).then_inc(k.experts_in, 16)

        normalise(k, "ln1", w.Wg1, k.wait_late, rows=g_rows, load=load_experts)
        route(k, "route", w.bg1, g_rows, r, sorted_dram)
        sorted_experts(k, "ffn1", W11, W21[:, :, :].rearrange("p n d -> p (n d)"), r, sorted_dram, made_dram)
        second.close()
        for b in range(BATCH):
            with ExitStack() as ctx:
                QT = sb(ctx, f"QT{b}", [P, PAIRS, SEQ], BF16)
                KT = sb(ctx, f"KT{b}", [P, PAIRS, SEQ], BF16)
                V = sb(ctx, f"V{b}", [P, SEQ // P, D])
                attn = sb(ctx, f"attn{b}", [P, SEQ // P, D])
                attention_operands(k, b, w, QT, KT, V, attn)
                softmax_attention(k, b, QT, KT, V, attn, gather if b == 0 else None)
                finish(k, b, w, attn, g_rows, r, out)


_TURNED = {"L1_attn_wq": "L1_attn_wqT", "L1_attn_wk": "L1_attn_wkT", "L1_attn_wv": "L1_attn_wvT", "L1_attn_wo": "L1_attn_woT"}


def kernel(**inputs):
    import numpy as _np
    import concourse.bacc as _bacc
    from concourse import mybir as _mybir
    from concourse.bass_utils import run_bass_kernel_spmd as _run

    nc = _bacc.Bacc("TRN2", target_bir_lowering=False, num_devices=1)
    arrays, args = {}, {}
    for name, a in inputs.items():
        a = _np.asarray(a)
        if name in _TURNED:
            name, a = _TURNED[name], a.T
        elif name == "L0_ffn_b1":
            name, a = "L0_ffn_b1T", a.reshape(-1, P).T
        a = _np.ascontiguousarray(a)
        arrays[f"in_{name}_dram"] = a
        args[name] = nc.dram_tensor(f"in_{name}_dram", a.shape, _mybir.dt.from_np(a.dtype), kind="ExternalInput").ap()
    out = nc.dram_tensor("out_dram", (BATCH, SEQ, D), F32, kind="ExternalOutput").ap()
    build(nc, args, out)
    r = _run(nc, [arrays], core_ids=[0])
    return r.results[0]["out_dram"]
```
